# Optimizing a Trainium2 kernel written in Bass

```python
import numpy as np
import jax
import jax.numpy as jnp

def _softmax(x, axis=-1):
    return jax.nn.softmax(x, axis=axis)
def _gelu(x):
    return jax.nn.gelu(x, approximate=True)
def _silu(x):
    return jax.nn.silu(x)
def _sigmoid(x):
    return jax.nn.sigmoid(x)
def _layernorm(x, axis=-1, eps=1e-5):
    m = jnp.mean(x, axis=axis, keepdims=True)
    v = jnp.var(x, axis=axis, keepdims=True)
    return (x - m) / jnp.sqrt(v + eps)
def _scatter_add(tgt, idx, src, axis=0):
    return tgt.at[idx].add(src)
def _segment_sum(src, seg, n):
    return jax.ops.segment_sum(src, seg, n)

kernel_name = 'mk_adj_ffn_d1_adj_256_a1fc56'

def setup_inputs(seed: int = 0):
    np.random.seed(seed)
    _w = jnp.asarray
    def _rec_inputs():
        import jax
        import jax.numpy as jnp
        _gk = jax.random.key(seed)
        x = -0.0005207 + 1.001 * jax.random.normal(jax.random.fold_in(_gk, 1), (128, 128, 256), jnp.float32)
        _a = jax.random.bernoulli(jax.random.fold_in(_gk, 2), 0.03125, (128, 128))
        _a = jnp.logical_or(_a, jnp.swapaxes(_a, -1, -2))
        _a = jnp.logical_or(_a, jnp.eye(128, dtype=bool))
        _af = _a.astype(jnp.float32)
        _af = _af * jax.random.uniform(jax.random.fold_in(_gk, 3), (128, 128), jnp.float32, 0.05, 32)
        adj = _af
        return x, adj
    x, adj = _rec_inputs()
    def _L0_gnn_setup():
        import jax, jax.numpy as jnp
        import numpy as np
        EPS_LN = 1e-05

        def _layernorm(x, g, b):
            mu = x.mean(-1, keepdims=True)
            var = ((x - mu) ** 2).mean(-1, keepdims=True)
            return (x - mu) / jnp.sqrt(var + EPS_LN) * g + b
        key = jax.random.key(seed)
        B, N, D, H = (4, 2048, 256, 4)
        hid = int(D * 2.0)
        ks = jax.random.split(key, 12)
        x = jax.random.normal(ks[0], (B, N, D), jnp.float32)
        Au = jax.random.uniform(ks[1], (N, N)) < 0.004
        A = jnp.logical_or(Au, Au.T)
        A = A.at[jnp.arange(N), jnp.arange(N)].set(False)
        Af = A.astype(jnp.float32)
        deg = Af.sum(axis=1)
        L = jnp.diag(deg) - Af
        adjacency = Af + jnp.eye(N, dtype=jnp.float32)
        s = lambda k, sh, f: jax.random.normal(k, sh, jnp.float32) * f
        sc = 1.0 / np.sqrt(D)
        Wc = s(ks[2], (D, D), sc)
        bc = jnp.zeros((D,), jnp.float32)
        Wq = s(ks[3], (D, D), sc)
        Wk = s(ks[4], (D, D), sc)
        Wv = s(ks[5], (D, D), sc)
        Wo = s(ks[6], (D, D), sc)
        bo = jnp.zeros((D,), jnp.float32)
        W1 = s(ks[7], (D, hid), sc)
        b1 = jnp.zeros((hid,), jnp.float32)
        W2 = s(ks[8], (hid, D), 1.0 / np.sqrt(hid))
        b2 = jnp.zeros((D,), jnp.float32)
        g1 = jnp.ones((D,), jnp.float32)
        be1 = jnp.zeros((D,), jnp.float32)
        g2 = jnp.ones((D,), jnp.float32)
        be2 = jnp.zeros((D,), jnp.float32)
        g3 = jnp.ones((D,), jnp.float32)
        be3 = jnp.zeros((D,), jnp.float32)
        return dict(x=x, L=L, adjacency=adjacency, Wc=Wc, bc=bc, g1=g1, be1=be1, Wq=Wq, Wk=Wk, Wv=Wv, Wo=Wo, bo=bo, g2=g2, be2=be2, W1=W1, b1=b1, W2=W2, b2=b2, g3=g3, be3=be3)
    _L0_gnn_all = _L0_gnn_setup()
    _L0_gnn_in = {k: v for k, v in _L0_gnn_all.items() if k in ('Wc', 'bc', 'g1', 'be1', 'Wq', 'Wk', 'Wv', 'Wo', 'bo', 'g2', 'be2', 'W1', 'b1', 'W2', 'b2', 'g3', 'be3', )}
    del _L0_gnn_all

    def _L0_ffn_setup():
        import jax, jax.numpy as jnp
        import numpy as np
        NUM_EXPERTS = 8
        TOP_K = 2
        B, S, D = (8, 8192, 256)

        def _moe(tokens, router_w, w1, b1, w2, b2):
            N = tokens.shape[0]
            E = router_w.shape[0]
            logits = tokens.astype(jnp.float32) @ router_w.astype(jnp.float32).T
            probs = jax.nn.softmax(logits, axis=-1)
            rw, re = jax.lax.top_k(probs, TOP_K)
            if TOP_K > 1:
                rw = rw / jnp.maximum(rw.sum(-1, keepdims=True), 1e-12)
            rw = rw.astype(tokens.dtype)
            combine = jnp.zeros((N, E), tokens.dtype).at[jnp.arange(N)[:, None], re].set(rw)
            out = tokens
            for e in range(E):
                h = jax.nn.gelu(tokens @ w1[e] + b1[e], approximate=False)
                y = h @ w2[e] + b2[e]
                out = out + combine[:, e:e + 1] * y
            return out
        key = jax.random.key(seed)
        ks = jax.random.split(key, 4)
        scale = 1.0 / np.sqrt(D).astype(np.float32)
        return {'input_embeddings': jax.random.normal(ks[0], (B, S, D), jnp.float32), 'router_w': jax.random.normal(ks[1], (NUM_EXPERTS, D), jnp.float32) * scale, 'w1': jax.random.normal(ks[2], (NUM_EXPERTS, D, D), jnp.float32) * scale, 'b1': jnp.zeros((NUM_EXPERTS, D), jnp.float32), 'w2': jax.random.normal(ks[3], (NUM_EXPERTS, D, D), jnp.float32) * scale, 'b2': jnp.zeros((NUM_EXPERTS, D), jnp.float32)}
    _L0_ffn_all = _L0_ffn_setup()
    _L0_ffn_in = {k: v for k, v in _L0_ffn_all.items() if k in ('router_w', 'w1', 'b1', 'w2', 'b2', )}
    del _L0_ffn_all

    return {
        "x": x,
        "adj": adj,
        "L0_gnn_Wc": _L0_gnn_in["Wc"],
        "L0_gnn_bc": _L0_gnn_in["bc"],
        "L0_gnn_g1": _L0_gnn_in["g1"],
        "L0_gnn_be1": _L0_gnn_in["be1"],
        "L0_gnn_Wq": _L0_gnn_in["Wq"],
        "L0_gnn_Wk": _L0_gnn_in["Wk"],
        "L0_gnn_Wv": _L0_gnn_in["Wv"],
        "L0_gnn_Wo": _L0_gnn_in["Wo"],
        "L0_gnn_bo": _L0_gnn_in["bo"],
        "L0_gnn_g2": _L0_gnn_in["g2"],
        "L0_gnn_be2": _L0_gnn_in["be2"],
        "L0_gnn_W1": _L0_gnn_in["W1"],
        "L0_gnn_b1": _L0_gnn_in["b1"],
        "L0_gnn_W2": _L0_gnn_in["W2"],
        "L0_gnn_b2": _L0_gnn_in["b2"],
        "L0_gnn_g3": _L0_gnn_in["g3"],
        "L0_gnn_be3": _L0_gnn_in["be3"],
        "L0_ffn_router_w": _L0_ffn_in["router_w"],
        "L0_ffn_w1": _L0_ffn_in["w1"],
        "L0_ffn_b1": _L0_ffn_in["b1"],
        "L0_ffn_w2": _L0_ffn_in["w2"],
        "L0_ffn_b2": _L0_ffn_in["b2"],
    }

def reference(x, adj, L0_gnn_Wc, L0_gnn_bc, L0_gnn_g1, L0_gnn_be1, L0_gnn_Wq, L0_gnn_Wk, L0_gnn_Wv, L0_gnn_Wo, L0_gnn_bo, L0_gnn_g2, L0_gnn_be2, L0_gnn_W1, L0_gnn_b1, L0_gnn_W2, L0_gnn_b2, L0_gnn_g3, L0_gnn_be3, L0_ffn_router_w, L0_ffn_w1, L0_ffn_b1, L0_ffn_w2, L0_ffn_b2):
    import jax
    import jax.numpy as jnp
    def _L0_gnn_ref(x, L, adjacency, Wc, bc, g1, be1, Wq, Wk, Wv, Wo, bo, g2, be2, W1, b1, W2, b2, g3, be3):
        import jax, jax.numpy as jnp
        import numpy as np
        EPS_LN = 1e-05

        def _layernorm(x, g, b):
            mu = x.mean(-1, keepdims=True)
            var = ((x - mu) ** 2).mean(-1, keepdims=True)
            return (x - mu) / jnp.sqrt(var + EPS_LN) * g + b
        B, N, D = x.shape
        H = 4
        hd = D // H
        eig = jnp.linalg.eigvalsh(L)
        lam_max = eig[-1] + 1e-08
        L_norm = 2.0 * L / lam_max - jnp.eye(N, dtype=L.dtype)
        xp = jnp.einsum('mn,bnf->bmf', L_norm, x)
        h = xp @ Wc + bc
        h = _layernorm(h, g1, be1)
        h = jax.nn.relu(h)
        x1 = h + x
        q = (x1 @ Wq).reshape(B, N, H, hd).transpose(0, 2, 1, 3)
        k = (x1 @ Wk).reshape(B, N, H, hd).transpose(0, 2, 1, 3)
        v = (x1 @ Wv).reshape(B, N, H, hd).transpose(0, 2, 1, 3)
        scores = jnp.einsum('bhnd,bhmd->bhnm', q, k) / np.sqrt(hd).astype(np.float32)
        scores = jnp.where(adjacency[None, None] > 0, scores, jnp.float32(-1000000000.0))
        attn = jax.nn.softmax(scores, axis=-1)
        o = jnp.einsum('bhnm,bhmd->bhnd', attn, v)
        o = o.transpose(0, 2, 1, 3).reshape(B, N, D)
        o = o @ Wo + bo
        x2 = _layernorm(x1 + o, g2, be2)
        m = jax.nn.gelu(x2 @ W1 + b1, approximate=False) @ W2 + b2
        return _layernorm(x2 + m, g3, be3)

    def _L0_ffn_ref(input_embeddings, router_w, w1, b1, w2, b2):
        import jax, jax.numpy as jnp
        import numpy as np
        NUM_EXPERTS = 8
        TOP_K = 2
        B, S, D = (8, 8192, 256)

        def _moe(tokens, router_w, w1, b1, w2, b2):
            N = tokens.shape[0]
            E = router_w.shape[0]
            logits = tokens.astype(jnp.float32) @ router_w.astype(jnp.float32).T
            probs = jax.nn.softmax(logits, axis=-1)
            rw, re = jax.lax.top_k(probs, TOP_K)
            if TOP_K > 1:
                rw = rw / jnp.maximum(rw.sum(-1, keepdims=True), 1e-12)
            rw = rw.astype(tokens.dtype)
            combine = jnp.zeros((N, E), tokens.dtype).at[jnp.arange(N)[:, None], re].set(rw)
            out = tokens
            for e in range(E):
                h = jax.nn.gelu(tokens @ w1[e] + b1[e], approximate=False)
                y = h @ w2[e] + b2[e]
                out = out + combine[:, e:e + 1] * y
            return out
        b, s, d = input_embeddings.shape
        tokens = input_embeddings.reshape(b * s, d)
        return _moe(tokens, router_w, w1, b1, w2, b2).reshape(b, s, d)

    x = x + _L0_gnn_ref(_layernorm(x, axis=-1), adj, adj, L0_gnn_Wc, L0_gnn_bc, L0_gnn_g1, L0_gnn_be1, L0_gnn_Wq, L0_gnn_Wk, L0_gnn_Wv, L0_gnn_Wo, L0_gnn_bo, L0_gnn_g2, L0_gnn_be2, L0_gnn_W1, L0_gnn_b1, L0_gnn_W2, L0_gnn_b2, L0_gnn_g3, L0_gnn_be3)
    x = x + _L0_ffn_ref(_layernorm(x, axis=-1), L0_ffn_router_w, L0_ffn_w1, L0_ffn_b1, L0_ffn_w2, L0_ffn_b2)
    return x


_drawn_inputs = setup_inputs


def setup_inputs(seed=0):
    import zlib

    import numpy as np

    out = dict(_drawn_inputs(seed))
    spreads = {'L0_gnn_bc': (0.0, 0.1),
     'L0_gnn_g1': (1.0, 0.2),
     'L0_gnn_be1': (0.0, 0.1),
     'L0_gnn_bo': (0.0, 0.1),
     'L0_gnn_g2': (1.0, 0.2),
     'L0_gnn_be2': (0.0, 0.1),
     'L0_gnn_b1': (0.0, 0.1),
     'L0_gnn_b2': (0.0, 0.1),
     'L0_gnn_g3': (1.0, 0.2),
     'L0_gnn_be3': (0.0, 0.1),
     'L0_ffn_b1': (0.0, 0.448),
     'L0_ffn_b2': (0.0, 0.306)}
    factors = {}
    for name, (base, spread) in spreads.items():
        noise = np.random.default_rng([zlib.crc32(name.encode()), seed]).standard_normal(out[name].shape)
        drawn = base * np.exp(spread * noise) if base else spread * noise
        out[name] = jnp.asarray(drawn.astype(out[name].dtype))
    for name, factor in factors.items():
        out[name] = (out[name] * factor).astype(out[name].dtype)
    return out
```

```python
from contextlib import ExitStack

import concourse.bass as bass
import numpy as np
from concourse import mybir

F32 = mybir.dt.float32
F16 = mybir.dt.float16
I32 = mybir.dt.int32
U32 = mybir.dt.uint32
ALU = mybir.AluOpType
ACT = mybir.ActivationFunctionType
AX_X = mybir.AxisListType.X
ds = bass.ds

P = 128
EPS = 1e-5
WS = 64.0
SQUARINGS = 25
NORM_EVERY = 3
KEEP = 3e38
PARTS = ((0, 0), (0, 1), (1, 0))


class Group:

    def __init__(self, eng, off, reg=None, cache=None):
        self.eng, self.off, self.reg = eng, off, reg
        self.cache = {} if cache is None else cache

    def back(self, k):
        return Group(self.eng, self.off - k, self.reg, self.cache)

    def par(self):
        return self.off % 2

    def n(self, k=0, mul=1, plus=0):
        if self.reg is None:
            return (self.off + k) * mul + plus
        key = ((self.off + k) * mul + plus, mul)
        if key not in self.cache:
            self.cache[key] = self.eng.snap(self.reg * mul + key[0])
            self.eng.to_reg(self.cache[key])
        return self.cache[key]

    def same(self, mul=1):
        return self.n(-self.par(), mul)

    def same_done(self, mul=1):
        return self.n(2 - self.par(), mul)

    def has(self, k):
        return self.reg is not None or self.off >= k

    def active(self, count):
        return self.reg is not None or 0 <= self.off < count


def own_wait(eng, over, semaphore, value):
    eng.wait_ge(over, 1)
    eng.wait_ge(semaphore, value)


def pipeline(eng, count, depth, tick, first):
    assert first % 2 == 0 and first >= depth - 1
    assert (count - first) % 2 == 0
    for u in range(first):
        tick(Group(eng, u))
    with eng.Fori(first, count - 1, 2) as i:
        cache = {}
        tick(Group(eng, 0, i, cache))
        tick(Group(eng, 1, i, cache))
    for u in range(count, count + depth - 1):
        tick(Group(eng, u))


def build_program(nc, x, adj, Wc, bc, g1, be1, Wq, Wk, Wv, Wo, bo, g2, be2, W1, b1, W2, b2, g3, be3,
                  router_w, mw1, mb1, mw2, mb2, out):
    NB, N, D = x.shape
    H = 4
    HD = D // H
    HID = W1.shape[1]
    E = router_w.shape[0]
    TOK = NB * N
    KC = D // P
    HC = HID // P
    T = 4
    NG = NB // T
    GT = T * P
    assert N == P and KC == 2 and H == 4 and HD == 64 and T == 4
    BLK = 256
    TB = BLK // P
    CAP = TOK + BLK
    NBLK = 2 * TOK // BLK + E
    ROWS = E * CAP + E * BLK
    assert ROWS < 1 << 24 and ROWS * D * 4 < 1 << 31
    MASKED = -1e9 * float(np.sqrt(HD))

    ctx = ExitStack()
    with ctx:
        def sb(name, shape, dt=F32):
            return ctx.enter_context(nc.sbuf_tensor(name, shape, dt))

        def sem(name):
            return ctx.enter_context(nc.semaphore(name))

        slots_t = nc.dram_tensor("expert_tokens", [ROWS, D], F32, kind="Internal").ap()
        slots_y = nc.dram_tensor("expert_outputs", [NBLK * BLK, D], F32, kind="Internal").ap()
        resid = nc.dram_tensor("residual", [NB, N, D], F32, kind="Internal").ap()

        ident = sb("ident", [P, P])
        ones = sb("ones", [P, P])
        ones_h = sb("ones_h", [P, P], F16)
        before_h = sb("before_h", [P, P], F16)
        eighth = sb("eighth", [P, E])
        zeros = sb("zeros", [P, TB * D])
        w_c = sb("w_c", [P, KC, D])
        w_o = sb("w_o", [P, KC, D])
        w_qkv = sb("w_qkv", [P, 3, 2, KC, D], F16)
        w_f1 = sb("w_f1", [P, 2, KC, HID], F16)
        w_f2 = sb("w_f2", [P, HC, D])
        w_r = sb("w_r", [P, KC, E])
        m_w1 = sb("m_w1", [P, E * 2 * KC * D], F16)
        m_w2 = sb("m_w2", [P, E * 2 * KC * D], F16)
        m_b1 = sb("m_b1", [P, E * KC])
        m_b2 = sb("m_b2", [P, E * D])
        f_b1 = sb("f_b1", [P, HC])
        rows = sb("rows", [P, 9, D])
        BC, G1, BE1, BO, G2, BE2, B2, G3, BE3 = range(9)
        EXP_LN = 6
        A = sb("A", [P, P])
        AT = sb("AT", [P, P])
        LT = sb("LT", [P, P])
        cap = sb("cap", [P, P])

        x_in = sb("x_in", [P, 2, T, D])
        x0 = sb("x0", [P, 2, T, D])
        xpT = sb("xpT", [P, KC, GT])
        hb = sb("hb", [P, T, D])
        x1 = sb("x1", [P, 2, T, D])
        x1s = sb("x1s", [P, 2, KC, GT], F16)
        qT = sb("qT", [P, 2, KC, GT])
        kT = sb("kT", [P, 2, KC, GT])
        v = sb("v", [P, 2, T, D])
        prob = sb("prob", [P, 2, 8, P])
        pT = sb("pT", [P, 8, P])
        oT = sb("oT", [P, KC, GT])
        yb = sb("yb", [P, T, D])
        x2 = sb("x2", [P, 2, T, D])
        x2s = sb("x2s", [P, 2, KC, GT], F16)
        hid = sb("hid", [P, HC, GT])
        zb = sb("zb", [P, T, D])
        x_res = sb("x_res", [P, T, D])
        r_out = sb("r_out", [P, T, D])
        t_out = sb("t_out", [P, 2, T, D])
        tT = sb("tT", [P, KC, GT])
        st = sb("st", [P, 5, T, 6])
        mv = sb("mv", [P, 5, T, 2])
        lnv = sb("lnv", [P, 5, T])
        root0 = sb("root0", [P, 5, T])
        eps = sb("eps", [P, 1])
        nh = sb("nh", [P, 5, T])
        nt = sb("nt", [P, 5, T])
        shifts = sb("shifts", [P, 5, T])
        rstd = sb("rstd", [P, 5, T])
        mx = sb("mx", [P, 2, 8])
        nmx = sb("nmx", [P, 2, 8])
        rsum = sb("rsum", [P, 2, 8])
        rinv = sb("rinv", [P, 2, 8])
        lg = sb("lg", [P, T, E])
        top = sb("top", [P, T, 8])
        topi = sb("topi", [P, T, 8], U32)
        topf = sb("topf", [P, 2, T])
        oneh = sb("oneh", [P, 2, T, E])
        picked = sb("picked", [P, T, E], F16)
        pos = sb("pos", [P, T, E])
        sel = sb("sel", [P, 2, T, E])
        slotf = sb("slotf", [P, 2, T])
        slot_now = sb("slot_now", [P, 2, 2, T], U32)
        count = sb("count", [P, E])
        slot_all = sb("slot_all", [P, 2 * NB])
        dtop = sb("dtop", [P, NB])
        idx2 = sb("idx2", [P, 2, 2, T], U32)
        biota = sb("biota", [P, NBLK])
        brow = yb[0:1, 0:2, 0:NBLK]
        hS = sb("hS", [P, 2, 2, KC, BLK], F16)
        tiny = sb("tiny", [P, 16])
        etab = sb("etab", [P, 16])
        etab_i = sb("etab_i", [P, 16], I32)
        blk_row = sb("blk_row", [1, NBLK], I32)
        blk_exp = sb("blk_exp", [1, NBLK], I32)
        pad_row = sb("pad_row", [1, E], I32)
        shift = xpT[:, 0, 0:2 * NB]
        moved = xpT[:, 0, 2 * NB:4 * NB]
        comb = oT[:, 0, 0:3 * NB].rearrange("p (i n) -> p i n", n=NB)

        D0 = ctx.enter_context(nc.psum_tensor("D0", [P, 1024], F32))
        D1 = ctx.enter_context(nc.psum_tensor("D1", [P, 1024], F32))
        D2 = ctx.enter_context(nc.psum_tensor("D2", [P, 1024], F32))
        D3 = ctx.enter_context(nc.psum_tensor("D3", [P, 1024], F32))

        stage = hid[:, :, :].rearrange("p a b -> p (a b)")
        S2 = hb[:, 0, 0:P]
        sabs = hb[:, 0, P:2 * P]
        sq = hb[:, 1, :].rearrange("p (i n) -> p i n", i=2)
        tS = (x1s, x2s)
        EIG_DVE = 3 + SQUARINGS + SQUARINGS // NORM_EVERY

        w_loaded = [sem(f"w_loaded{i}") for i in range(3)]
        stage_loaded = [sem(f"stage_loaded{i}") for i in range(2)]
        stage_hi = sem("stage_hi")
        stage_lo = sem("stage_lo")
        const_ready = sem("const_ready")
        eig_pe = sem("eig_pe")
        eig_dve = sem("eig_dve")
        eig_act = sem("eig_act")
        lt_ready = sem("lt_ready")
        pad_zeroed = sem("pad_zeroed")
        x_loaded = [sem(f"x_loaded{i}") for i in range(2)]
        stats_ready = [sem(f"stats_ready{i}") for i in range(5)]
        aggr_ready = [sem(f"aggr_ready{i}") for i in range(5)]
        ln_ready = [sem(f"ln_ready{i}") for i in range(5)]
        root_ready = [sem(f"root_ready{i}") for i in range(5)]
        refine_step = [sem(f"refine_step{i}") for i in range(5)]
        white_ready = {i: sem(f"white_ready{i}") for i in (1, 2, 3)}
        gained = {i: sem(f"gained{i}") for i in (1, 2, 3)}
        filled = sem("filled")
        x0_ready = sem("x0_ready")
        xp_done = sem("xp_done")
        xpT_ready = sem("xpT_ready")
        h_done = sem("h_done")
        hb_ready = sem("hb_ready")
        hb_normed = sem("hb_normed")
        x1_ready = sem("x1_ready")
        x1T_done = sem("x1T_done")
        x1hi_ready = sem("x1hi_ready")
        x1lo_ready = sem("x1lo_ready")
        q_done = sem("q_done")
        q_ready = sem("q_ready")
        k_done = sem("k_done")
        k_ready = sem("k_ready")
        v_done = sem("v_done")
        v_ready = sem("v_ready")
        x1b_ready = sem("x1b_ready")
        sc_done = [sem(f"sc_done{i}") for i in range(2)]
        sc_capped = [sem(f"sc_capped{i}") for i in range(2)]
        mx_ready = [sem(f"mx_ready{i}") for i in range(2)]
        nmx_ready = [sem(f"nmx_ready{i}") for i in range(2)]
        exp_done = [sem(f"exp_done{i}") for i in range(2)]
        rinv_ready = [sem(f"rinv_ready{i}") for i in range(2)]
        prob_ready = [sem(f"prob_ready{i}") for i in range(2)]
        pT_done = [sem(f"pT_done{i}") for i in range(2)]
        pT_ready = [sem(f"pT_ready{i}") for i in range(2)]
        pv_done = [sem(f"pv_done{i}") for i in range(2)]
        oT_ready = [sem(f"oT_ready{i}") for i in range(2)]
        wo_done = sem("wo_done")
        yb_ready = sem("yb_ready")
        x2_ready = sem("x2_ready")
        x2T_done = sem("x2T_done")
        x2b_ready = sem("x2b_ready")
        x2hi_ready = sem("x2hi_ready")
        x2lo_ready = sem("x2lo_ready")
        f1_done = [sem(f"f1_done{i}") for i in range(2)]
        hid_ready = [sem(f"hid_ready{i}") for i in range(2)]
        f2_done = sem("f2_done")
        zb_ready = sem("zb_ready")
        xres_loaded = sem("xres_loaded")
        xres_ready = sem("xres_ready")
        xn_ready = sem("xn_ready")
        t_ready = sem("t_ready")
        r_ready = sem("r_ready")
        r_stored = sem("r_stored")
        tT_done = sem("tT_done")
        tT_ready = sem("tT_ready")
        lg_done = sem("lg_done")
        lg_ready = sem("lg_ready")
        top_ready = sem("top_ready")
        topi_ready = sem("topi_ready")
        topf_ready = sem("topf_ready")
        oneh_ready = sem("oneh_ready")
        picked_ready = sem("picked_ready")
        rank_done = sem("rank_done")
        pos_ready = sem("pos_ready")
        sel_ready = sem("sel_ready")
        slotf_ready = sem("slotf_ready")
        slot_ready = sem("slot_ready")
        count_ready = sem("count_ready")
        scattered = [sem(f"scattered{i}") for i in range(2)]
        table_step = sem("table_step")
        table_ready = sem("table_ready")
        comb_act = sem("comb_act")
        comb_ready = sem("comb_ready")
        mt_loaded = [sem(f"mt_loaded{i}") for i in range(2)]
        mt_done = sem("mt_done")
        mt_hi = sem("mt_hi")
        mt_lo = sem("mt_lo")
        m1_done = sem("m1_done")
        mh_gelu = sem("mh_gelu")
        mh_hi = sem("mh_hi")
        mh_lo = sem("mh_lo")
        m2_done = sem("m2_done")
        y_ready = sem("y_ready")
        y_stored = [sem(f"y_stored{i}") for i in range(2)]
        idx_ready = sem("idx_ready")
        gathered = [sem(f"gathered{i}") for i in range(2)]
        rl_loaded = [sem(f"rl_loaded{i}") for i in range(2)]
        mix1 = sem("mix1")
        mix2 = sem("mix2")
        out_stored = [sem(f"out_stored{i}") for i in range(2)]

        x_v = x.rearrange("b n f -> n b f")
        out_v = out.rearrange("b n f -> n b f")
        resid_v = resid.rearrange("b n f -> n b f")
        slots_t_v = slots_t.rearrange("(b p) f -> p b f", p=P)
        slots_y_v = slots_y.rearrange("(b p) f -> p b f", p=P)
        mw1_v = mw1.rearrange("e (c p) n -> p e c n", p=P)
        mw2_v = mw2.rearrange("e (c p) n -> p e c n", p=P)

        def split_jobs():
            jobs = []
            for i, w in enumerate((Wq, Wk, Wv)):
                jobs.append((w.rearrange("(c p) n -> p c n", p=P), [P, KC, D],
                             w_qkv[:, i, 0], w_qkv[:, i, 1]))
            jobs.append((W1.rearrange("(c p) n -> p c n", p=P), [P, KC, HID], w_f1[:, 0], w_f1[:, 1]))
            for src, dst in ((mw1_v, m_w1), (mw2_v, m_w2)):
                d = dst[:, :].rearrange("p (e s c n) -> p e s c n", e=E, s=2, c=KC)
                for e in range(0, E, 2):
                    jobs.append((src[:, e:e + 2], [P, 2, KC, D], d[:, e:e + 2, 0], d[:, e:e + 2, 1]))
            return jobs

        JOBS = split_jobs()

        def staged(n):
            shape = JOBS[n][1]
            cols = int(np.prod(shape[1:]))
            flat = stage[:, (n % 2) * 1024:(n % 2) * 1024 + cols]
            if len(shape) == 3:
                return flat.rearrange("p (a b) -> p a b", a=shape[1])
            return flat.rearrange("p (a b c) -> p a b c", a=shape[1], b=shape[2])

        block = ctx.enter_context(nc.Block())

        @block.sync
        def _(sp):
            sp.dma_start(A[:, :], adj).then_inc(w_loaded[0], 16)
            for i, r in enumerate((bc, g1, be1, bo, g2, be2, b2, g3, be3)):
                sp.dma_start(rows[:, i, :], r.partition_broadcast(P)).then_inc(w_loaded[1], 16)
            sp.dma_start(w_c[:, :, :], Wc.rearrange("(c p) n -> p c n", p=P)).then_inc(w_loaded[1], 16)
            sp.dma_start(f_b1[:, :], b1.rearrange("(c p) -> p c", p=P), allow_slow_non_contiguous=True).then_inc(w_loaded[1], 16)
            for n, (src, _, _, _) in enumerate(JOBS):
                if n >= 2:
                    sp.wait_ge(stage_lo, n - 1)
                sp.dma_start(staged(n), src).then_inc(stage_loaded[n % 2], 16)
            sp.dma_start(w_o[:, :, :], Wo.rearrange("(c p) n -> p c n", p=P)).then_inc(w_loaded[2], 16)
            sp.dma_start(w_f2[:, :, :], W2.rearrange("(c p) n -> p c n", p=P)).then_inc(w_loaded[2], 16)
            for c in range(KC):
                sp.dma_start(w_r[:, c, :], router_w[:, c * P:(c + 1) * P].rearrange("e p -> p e"), allow_slow_non_contiguous=True)\
                  .then_inc(w_loaded[2], 16)
            sp.dma_start(m_b1[:, :], mb1.rearrange("e (c p) -> p (e c)", p=P), allow_slow_non_contiguous=True).then_inc(w_loaded[2], 16)
            sp.dma_start(m_b2[:, :], mb2.rearrange("e n -> (e n)").partition_broadcast(P))\
              .then_inc(w_loaded[2], 16)
            sp.wait_ge(const_ready, 1)
            for i in range(E):
                b = (E * CAP + i * BLK) // P
                sp.dma_start(slots_t_v[:, b:b + TB, :],
                             zeros[:, :].rearrange("p (b f) -> p b f", b=TB)).then_inc(pad_zeroed, 16)

            def tick(u):
                g = u
                if g.active(NG):
                    if g.has(2):
                        sp.wait_ge(x0_ready, g.n(-1))
                    sp.dma_start(x_in[:, g.par()], x_v[:, ds(g.n(0, T), T), :])\
                      .then_inc(x_loaded[g.par()], 16)
                g = u.back(3)
                if g.active(NG):
                    if g.has(1):
                        sp.wait_ge(xn_ready, g.n())
                    sp.dma_start(x_res[:, :, :], x_v[:, ds(g.n(0, T), T), :]).then_inc(xres_loaded, 16)
                g = u.back(4)
                if g.active(NG):
                    sp.wait_ge(r_ready, g.n(1))
                    sp.dma_start(resid_v[:, ds(g.n(0, T), T), :], r_out[:, :, :]).then_inc(r_stored, 16)

            pipeline(sp, NG, 5, tick, 6)

            sp.wait_ge(scattered[0], 16 * T * NG)
            sp.wait_ge(scattered[1], 16 * T * NG)
            sp.wait_ge(table_ready, 1)
            for e in range(E):
                row = sp.value_load(pad_row[0:1, e:e + 1], min_val=e * CAP, max_val=e * CAP + TOK)
                sp.dma_start(slots_t[ds(row, BLK), :].rearrange("(b p) f -> p b f", p=P),
                             zeros[:, :].rearrange("p (b f) -> p b f", b=TB)).then_inc(pad_zeroed, 16)
            sp.wait_ge(pad_zeroed, 16 * 2 * E)
            sp.wait_ge(comb_ready, 1)

            def moe_tick(u):
                b = u
                if b.active(NBLK):
                    if b.has(2):
                        sp.wait_ge(mt_done, b.n(-1))
                    row = sp.value_load(blk_row[0:1, ds(b.n(), 1)], min_val=0, max_val=ROWS - BLK)
                    sp.dma_start(t_out[:, b.par(), 0:TB, :],
                                 slots_t[ds(row, BLK), :].rearrange("(b p) f -> p b f", p=P))\
                      .then_inc(mt_loaded[b.par()], 16)
                b = u.back(4)
                if b.active(NBLK):
                    sp.wait_ge(y_ready, b.n(1))
                    sp.dma_start(slots_y_v[:, ds(b.n(0, TB), TB), :], x2[:, b.par(), 0:TB, :]).then_inc(y_stored[b.par()], 16)

            pipeline(sp, NBLK, 5, moe_tick, 6)

            sp.wait_ge(r_stored, 16 * NG)

            def mix_tick(u):
                g = u
                if g.active(NG):
                    if g.has(2):
                        sp.wait_ge(mix2, g.n(-1))
                    sp.dma_start(x_in[:, g.par()], resid_v[:, ds(g.n(0, T), T), :])\
                      .then_inc(rl_loaded[g.par()], 16)
                g = u.back(1)
                if g.active(NG):
                    sp.wait_ge(mix2, g.n(1))
                    sp.dma_start(out_v[:, ds(g.n(0, T), T), :], x0[:, g.par()])\
                      .then_inc(out_stored[g.par()], 16)

            pipeline(sp, NG, 2, mix_tick, 4)
            sp.wait_ge(out_stored[0], 16 * NG // 2)
            sp.wait_ge(out_stored[1], 16 * NG // 2)

        @block.gpsimd
        def _(pool):
            pool.memset(zeros[:, :], 0.0)
            pool.memset(ones[:, :], 1.0)
            pool.memset(ones_h[:, :], 1.0)
            pool.memset(before_h[:, :], 1.0)
            pool.memset(ident[:, :], 0.0)
            pool.memset(eps[:, :], EPS)
            pool.iota(eighth[:, :], [[1, E]], base=0, channel_multiplier=0,
                      allow_small_or_imprecise_dtypes=True)
            pool.iota(biota[:, :], [[1, NBLK]], base=0, channel_multiplier=0,
                      allow_small_or_imprecise_dtypes=True)
            pool.iota(count[:, :], [[CAP, E]], base=0, channel_multiplier=0,
                      allow_small_or_imprecise_dtypes=True).then_inc(filled, 1)
            pool.wait_ge(filled, 1)
            pool.affine_select(out=before_h[:, :], in_=before_h[:, :], compare_op=ALU.is_gt, fill=0.0,
                               base=0, pattern=[[1, P]], channel_multiplier=-1)
            pool.affine_select(out=ident[:, :], in_=ident[:, :], compare_op=ALU.not_equal, fill=1.0,
                               base=0, pattern=[[-1, P]], channel_multiplier=1).then_inc(const_ready, 1)

            def add_row(dst, i):
                return pool.tensor_tensor(dst, dst, rows[:, i].unsqueeze(1).to_broadcast([P, T, D]), ALU.add)

            def normalise(g, jj):
                pool.wait_ge(rinv_ready[jj], g.n(1))
                pool.tensor_tensor(prob[:, jj], prob[:, jj],
                                   rinv[:, jj].unsqueeze(2).to_broadcast([P, 8, P]), ALU.mult)\
                    .then_inc(prob_ready[jj], 1)

            def tick(u):
                m0, m1, m2, m3, m4 = (u.back(k) for k in range(5))
                if m3.active(NG):
                    pool.wait_ge(x2T_done, m3.n(1))
                    add_row(x2[:, m3.par()], B2).then_inc(x2b_ready, 1)
                if m2.active(NG):
                    normalise(m2, 0)
                    pool.wait_ge(x1T_done, m2.n(1))
                    add_row(x1[:, m2.par()], BO).then_inc(x1b_ready, 1)
                if m3.active(NG):
                    pool.wait_ge(xres_loaded, m3.n(1, 16))
                    add_row(x_res[:, :, :], BE3).then_inc(xres_ready, 1)
                if m2.active(NG):
                    normalise(m2, 1)
                if m4.active(NG):
                    own_wait(pool, const_ready, slot_ready, m4.n(1))
                    for j in range(T):
                        for k in range(2):
                            pool.indirect_dma_start(
                                out=slots_t, in_=t_out[:, m4.par(), j, :], in_offset=None,
                                out_offset=bass.IndirectOffsetOnAxis(ap=slot_now[:, m4.par(), k, j:j + 1],
                                                                     axis=0))\
                                .then_inc(scattered[m4.par()], 16)
                if m3.active(NG):
                    pool.wait_ge(t_ready, m3.n(1))
                    if m3.has(1):
                        pool.wait_ge(r_stored, m3.n(0, 16))
                    pool.tensor_tensor(r_out[:, :, :], zb[:, :, :], t_out[:, m3.par()], ALU.add)\
                        .then_inc(r_ready, 1)

            pool.wait_ge(w_loaded[1], 16 * 11)
            pipeline(pool, NG, 5, tick, 6)

            pool.wait_ge(y_stored[0], 16 * NBLK // 2)
            pool.wait_ge(y_stored[1], 16 * NBLK // 2)

            def mix_tick(u):
                g = u
                if g.active(NG):
                    indexed, mixed = g.n(1), g.n(-1)
                    own_wait(pool, const_ready, idx_ready, indexed)
                    if g.has(2):
                        pool.wait_ge(mix2, mixed)
                    for j in range(T):
                        for k, dst in enumerate((x1, x2)):
                            pool.indirect_dma_start(
                                out=dst[:, g.par(), j, :], out_offset=None, in_=slots_y,
                                in_offset=bass.IndirectOffsetOnAxis(ap=idx2[:, g.par(), k, j:j + 1], axis=0))\
                                .then_inc(gathered[g.par()], 16)

            pipeline(pool, NG, 1, mix_tick, 2)

        @block.scalar
        def _(act):
            act.wait_ge(eig_dve, 1)
            act.activation(sabs[:, :], S2[:, :], ACT.Abs, accum_out=tiny[:, 0:1]).then_inc(eig_act, 1)
            for n, (_, _, hi, _) in enumerate(JOBS):
                act.wait_ge(stage_loaded[n % 2], 16 * (n // 2 + 1))
                act.activation(hi, staged(n), ACT.Copy, scale=WS).then_inc(stage_hi, 1)

            def flat(t):
                return t.rearrange("p a b -> p (a b)")

            def exps(g, jj):
                act.wait_ge(nmx_ready[jj], g.n(1))
                for i in range(8):
                    last = act.activation(prob[:, jj, i], prob[:, jj, i], ACT.Exp, bias=nmx[:, jj, i:i + 1],
                                          scale=float(1 / np.sqrt(HD)), accum_out=rsum[:, jj, i:i + 1])
                last.then_inc(exp_done[jj], 1)

            def gelus(g, half):
                act.wait_ge(f1_done[half], g.n(1))
                for i in range(2):
                    c = 2 * half + i
                    last = act.activation(hid[:, c], D3[:, i * 512:(i + 1) * 512], ACT.Gelu,
                                          bias=f_b1[:, c:c + 1], scale=1 / WS)
                last.then_inc(hid_ready[half], 1)

            def load_tables(which):
                act.add_instruction(mybir.InstLoadActFuncSet(
                    act_func_set_id=which, name=nc.get_next_instruction_name(), engine=act.engine))

            def root(g, k):
                act.wait_ge(aggr_ready[k], g.n(1))
                act.activation(lnv[:, k], mv[:, k, :, 1], ACT.Ln, bias=eps[:, :]).then_inc(ln_ready[k], 1)
                act.wait_ge(ln_ready[k], g.n(1))
                act.activation(root0[:, k], lnv[:, k], ACT.Exp, scale=-0.5).then_inc(root_ready[k], 1)

            def evac_p(g, jj):
                act.wait_ge(pT_done[jj], g.n(1))
                act.activation(flat(pT[:, :, :]), D2[:, :], ACT.Copy).then_inc(pT_ready[jj], 1)

            def evac_o(g, jj):
                act.wait_ge(pv_done[jj], g.n(1))
                act.activation(oT[:, :, jj * 256:(jj + 1) * 256],
                               D2[:, 0:512].rearrange("p (c n) -> p c n", c=KC), ACT.Copy)\
                   .then_inc(oT_ready[jj], 1)

            def evac(g, bank, done, dst, ready, scale):
                act.wait_ge(done, g.n(1))
                act.activation(dst, bank[:, :], ACT.Copy, scale=scale).then_inc(ready, 1)

            def whiten(g, k, dst, src, ready):
                act.wait_ge(refine_step[k], g.n(1, 4))
                for j in range(T):
                    last = act.activation(dst[:, j], src[:, j], ACT.Identity, bias=shifts[:, k, j:j + 1],
                                          scale=rstd[:, k, j:j + 1])
                last.then_inc(ready, 1)

            def tick(u):
                m0, m1, m2, m3, m4 = (u.back(k) for k in range(5))
                if m4.active(NG):
                    evac(m4, D2, tT_done, flat(tT[:, :, :]), tT_ready, 1.0)
                if m3.active(NG):
                    evac(m3, D3, x2T_done, flat(x2s[:, 0]), x2hi_ready, 1.0)
                if m1.active(NG):
                    evac(m1, D0, xp_done, flat(xpT[:, :, :]), xpT_ready, 1.0)
                if m2.active(NG):
                    exps(m2, 0)
                if m3.active(NG):
                    gelus(m3, 0)
                    gelus(m3, 1)
                    load_tables(EXP_LN)
                if m1.active(NG):
                    root(m1, 1)
                if m0.active(NG):
                    root(m0, 0)
                if m1.active(NG):
                    whiten(m1, 1, hb, hb, white_ready[1])
                if m2.active(NG):
                    exps(m2, 1)
                    evac_p(m2, 0)
                if m1.active(NG):
                    evac(m1, D0, x1T_done, flat(x1s[:, 0]), x1hi_ready, 1.0)
                if m2.active(NG):
                    evac_o(m2, 0)
                if m3.active(NG):
                    root(m3, 3)
                if m2.active(NG):
                    evac_p(m2, 1)
                if m3.active(NG):
                    whiten(m3, 3, zb, zb, white_ready[3])
                if m2.active(NG):
                    evac_o(m2, 1)
                if m1.active(NG):
                    evac(m1, D0, q_done, flat(qT[:, m1.par()]), q_ready, 1 / WS)
                if m3.active(NG):
                    root(m3, 4)
                if m0.active(NG):
                    whiten(m0, 0, x0[:, m0.par()], x_in[:, m0.par()], x0_ready)
                if m1.active(NG):
                    evac(m1, D0, k_done, flat(kT[:, m1.par()]), k_ready, 1 / WS)
                if m2.active(NG):
                    root(m2, 2)
                    whiten(m2, 2, yb, yb, white_ready[2])
                if m3.active(NG):
                    if m3.has(2):
                        act.wait_ge(scattered[m3.par()], m3.same(64))
                    whiten(m3, 4, t_out[:, m3.par()], zb, t_ready)
                if m1.active(NG):
                    evac(m1, D0, v_done, flat(v[:, m1.par()]), v_ready, 1 / WS)

            load_tables(EXP_LN)
            act.wait_ge(w_loaded[1], 16 * 11)
            pipeline(act, NG, 5, tick, 6)

            act.wait_ge(table_ready, 1)
            act.activation(comb[:, 0, :], dtop[:, :], ACT.Exp).then_inc(comb_act, 1)
            act.wait_ge(w_loaded[2], 16 * 6)

            def moe_tick(u):
                b = u.back(1)
                if b.active(NBLK):
                    act.wait_ge(mt_done, b.n(1))
                    act.activation(tS[b.par()][:, 0, :, 0:BLK],
                                   D0[:, b.par() * 512:(b.par() + 1) * 512].rearrange("p (c n) -> p c n", c=KC),
                                   ACT.Copy).then_inc(mt_hi, 1)
                b = u.back(2)
                if b.active(NBLK):
                    e = act.value_load(blk_exp[0:1, ds(b.n(), 1)], min_val=0, max_val=E - 1)
                    act.wait_ge(m1_done, b.n(1))
                    for m in range(KC):
                        last = act.activation(
                            hid[:, 2 * b.par() + m, 0:BLK],
                            D1[:, b.par() * 512 + m * BLK:b.par() * 512 + (m + 1) * BLK],
                            ACT.Gelu, bias=m_b1[:, ds(e * KC + m, 1)], scale=1 / WS)
                    last.then_inc(mh_gelu, 1)

            pipeline(act, NBLK, 5, moe_tick, 6)

        @block.vector
        def _(dve):
            chain = [0]

            def link(ins):
                chain[0] += 1
                ins.then_inc(table_step, 1)
                dve.wait_ge(table_step, chain[0])

            pe_n, jobs = [0], iter(range(len(JOBS)))

            def pe_step():
                pe_n[0] += 1
                dve.wait_ge(eig_pe, pe_n[0])

            def split_lo():
                n = next(jobs, None)
                if n is None:
                    return
                _, _, hi, lo = JOBS[n]
                dve.wait_ge(stage_hi, n + 1)
                s = staged(n)
                if len(s.shape) == 3:
                    dve.scalar_tensor_tensor(out=lo, in0=s, scalar=WS, in1=hi, op0=ALU.mult,
                                             op1=ALU.subtract).then_inc(stage_lo, 1)
                else:
                    for i in range(2):
                        last = dve.scalar_tensor_tensor(out=lo[:, i], in0=s[:, i], scalar=WS, in1=hi[:, i],
                                                        op0=ALU.mult, op1=ALU.subtract)
                    last.then_inc(stage_lo, 1)

            dve.wait_ge(w_loaded[0], 16)
            pe_step()
            link(dve.tensor_copy(AT[:, :], D3[:, 0:P]))
            dve.tensor_tensor(S2[:, :], A[:, :], AT[:, :], ALU.add).then_inc(eig_dve, 1)
            link(dve.tensor_scalar(cap[:, :], A[:, :], 0.0, KEEP, ALU.is_gt, ALU.mult))
            link(dve.tensor_scalar(cap[:, :], cap[:, :], MASKED, None, ALU.add))
            pe_step()
            link(dve.reduce_max(tiny[0:1, 1:2], D3[0:1, P:2 * P], AX_X))
            dve.tensor_scalar(tiny[0:1, 2:3], tiny[0:1, 1:2], 1e-30, None, ALU.max).then_inc(eig_dve, 1)
            pe_step()
            link(dve.tensor_copy(tiny[:, 3:4], D3[:, 256:257]))
            link(dve.reciprocal(tiny[:, 4:5], tiny[:, 3:4]))
            link(dve.scalar_tensor_tensor(out=sq[:, 0], in0=ident[:, :], scalar=tiny[:, 3:4], in1=S2[:, :],
                                          op0=ALU.mult, op1=ALU.add))
            dve.tensor_scalar(sq[:, 0], sq[:, 0], tiny[:, 4:5], 0.5, ALU.mult, ALU.mult).then_inc(eig_dve, 1)
            for i in range(SQUARINGS):
                split_lo()
                pe_step()
                src, dst = D2[:, (i % 2) * 512:(i % 2) * 512 + P], sq[:, (i + 1) % 2]
                if i % NORM_EVERY == NORM_EVERY - 1:
                    dve.tensor_tensor_reduce(sabs[:, :], src, ident[:, :], 1.0, 0.0, ALU.mult, ALU.add,
                                             tiny[:, 5:6]).then_inc(eig_dve, 1)
                    pe_step()
                    link(dve.reciprocal(tiny[:, 6:7], D3[:, 256:257]))
                    dve.tensor_scalar(dst, src, tiny[:, 6:7], None, ALU.mult).then_inc(eig_dve, 1)
                else:
                    dve.tensor_copy(dst, src).then_inc(eig_dve, 1)
            for _ in range(len(JOBS)):
                split_lo()
            last_sq = sq[:, SQUARINGS % 2]
            dve.wait_ge(eig_dve, EIG_DVE)
            link(dve.tensor_tensor_reduce(sabs[:, :], last_sq, S2[:, :], 1.0, 0.0, ALU.mult, ALU.add,
                                          tiny[:, 8:9]))
            dve.tensor_tensor_reduce(sabs[:, :], last_sq, ident[:, :], 1.0, 0.0, ALU.mult, ALU.add,
                                     tiny[:, 9:10]).then_inc(eig_dve, 1)
            pe_step()
            link(dve.tensor_copy(tiny[:, 10:12], D3[:, 256:258]))
            link(dve.reciprocal(tiny[:, 12:13], tiny[:, 11:12]))
            link(dve.scalar_tensor_tensor(out=tiny[:, 13:14], in0=tiny[:, 10:11], scalar=0.5,
                                          in1=tiny[:, 12:13], op0=ALU.mult, op1=ALU.mult))
            link(dve.tensor_scalar(tiny[:, 14:15], tiny[:, 13:14], 1e-8, 0.5, ALU.add, ALU.mult))
            link(dve.reciprocal(tiny[:, 15:16], tiny[:, 14:15]))
            dve.scalar_tensor_tensor(out=LT[:, :], in0=AT[:, :], scalar=tiny[:, 15:16], in1=ident[:, :],
                                     op0=ALU.mult, op1=ALU.subtract).then_inc(lt_ready, 1)

            def stats(g, k, src):
                for j in range(T):
                    last = dve.bn_stats(st[:, k, j], src[:, j])
                last.then_inc(stats_ready[k], 1)
                own_wait(dve, const_ready, stats_ready[k], g.n(1))
                for j in range(T):
                    last = dve.bn_aggr(mv[:, k, j], st[:, k, j])
                last.then_inc(aggr_ready[k], 1)

            def refine(g, k):
                dve.wait_ge(aggr_ready[k], g.n(1))
                dve.tensor_scalar(nh[:, k], mv[:, k, :, 1], EPS, -0.5, ALU.add, ALU.mult)
                dve.wait_ge(root_ready[k], g.n(1))
                dve.tensor_tensor(nt[:, k], root0[:, k], root0[:, k], ALU.mult).then_inc(refine_step[k], 1)
                dve.wait_ge(refine_step[k], g.n(0, 4, 1))
                dve.tensor_tensor(nt[:, k], nt[:, k], nh[:, k], ALU.mult).then_inc(refine_step[k], 1)
                dve.wait_ge(refine_step[k], g.n(0, 4, 2))
                dve.scalar_tensor_tensor(out=rstd[:, k], in0=nt[:, k], scalar=1.5, in1=root0[:, k],
                                         op0=ALU.add, op1=ALU.mult).then_inc(refine_step[k], 1)
                dve.wait_ge(refine_step[k], g.n(0, 4, 3))
                dve.scalar_tensor_tensor(out=shifts[:, k], in0=mv[:, k, :, 0], scalar=-1.0, in1=rstd[:, k],
                                         op0=ALU.mult, op1=ALU.mult).then_inc(refine_step[k], 1)

            def gain(g, buf, k, i):
                dve.wait_ge(white_ready[k], g.n(1))
                dve.tensor_tensor(buf[:, :, :], buf[:, :, :], rows[:, i].unsqueeze(1).to_broadcast([P, T, D]),
                                  ALU.mult).then_inc(gained[k], 1)
                dve.wait_ge(gained[k], g.n(1))

            def tiles(t):
                return t.rearrange("p (j n) -> p j n", j=T)

            def capped(g, jj):
                dve.wait_ge(sc_done[jj], g.n(1))
                dve.tensor_tensor(prob[:, jj], D1[:, :].rearrange("p (a m) -> p a m", m=P),
                                  cap[:, :].unsqueeze(1).to_broadcast([P, 8, P]), ALU.min)\
                   .then_inc(sc_capped[jj], 1)

            def maxima(g, jj):
                dve.wait_ge(sc_capped[jj], g.n(1))
                dve.tensor_reduce(mx[:, jj], prob[:, jj], AX_X, ALU.max).then_inc(mx_ready[jj], 1)
                dve.wait_ge(mx_ready[jj], g.n(1))
                dve.tensor_scalar(nmx[:, jj], mx[:, jj], -float(1 / np.sqrt(HD)), None, ALU.mult)\
                   .then_inc(nmx_ready[jj], 1)

            def inverse_sums(g, jj):
                dve.wait_ge(exp_done[jj], g.n(1))
                dve.reciprocal(rinv[:, jj], rsum[:, jj]).then_inc(rinv_ready[jj], 1)

            def low(g, bank, hi_ready, parts, ready):
                dve.wait_ge(hi_ready, g.n(1))
                dve.tensor_tensor(parts[:, 1].rearrange("p a b -> p (a b)"), bank[:, :],
                                  parts[:, 0].rearrange("p a b -> p (a b)"), ALU.subtract).then_inc(ready, 1)

            def choose(g):
                dve.wait_ge(lg_done, g.n(1))
                dve.tensor_copy(lg[:, :, :], D2[:, 0:T * E].rearrange("p (j e) -> p j e", e=E))\
                   .then_inc(lg_ready, 1)
                own_wait(dve, const_ready, lg_ready, g.n(1))
                for j in range(T):
                    last = dve.max(top[:, j], lg[:, j])
                last.then_inc(top_ready, 1)
                own_wait(dve, const_ready, top_ready, g.n(1))
                for j in range(T):
                    last = dve.max_index(topi[:, j], top[:, j], lg[:, j])
                last.then_inc(topi_ready, 1)
                dve.tensor_tensor(dtop[:, ds(g.n(0, T), T)], top[:, :, 1], top[:, :, 0], ALU.subtract)
                dve.wait_ge(topi_ready, g.n(1))
                dve.tensor_copy(topf[:, :, :], topi[:, :, 0:2].rearrange("p j k -> p k j"))\
                   .then_inc(topf_ready, 1)
                dve.wait_ge(topf_ready, g.n(1))
                for k in range(2):
                    last = dve.tensor_tensor(oneh[:, k], eighth[:, :].unsqueeze(1).to_broadcast([P, T, E]),
                                             topf[:, k].unsqueeze(2).to_broadcast([P, T, E]), ALU.is_equal)
                last.then_inc(oneh_ready, 1)
                dve.wait_ge(oneh_ready, g.n(1))
                dve.tensor_tensor(picked[:, :, :], oneh[:, 0], oneh[:, 1], ALU.add).then_inc(picked_ready, 1)

            def place(g):
                dve.wait_ge(rank_done, g.n(1))
                dve.tensor_tensor(pos[:, :, :], D2[:, 512:512 + T * E].rearrange("p (j e) -> p j e", e=E),
                                  count[:, :].unsqueeze(1).to_broadcast([P, T, E]), ALU.add)\
                   .then_inc(pos_ready, 1)
                dve.wait_ge(pos_ready, g.n(1))
                for k in range(2):
                    last = dve.tensor_tensor(sel[:, k], oneh[:, k], pos[:, :, :], ALU.mult)
                last.then_inc(sel_ready, 1)
                dve.tensor_tensor(count[:, :], count[:, :], D2[:, 512 + T * E:512 + (T + 1) * E], ALU.add)\
                   .then_inc(count_ready, 1)
                dve.wait_ge(sel_ready, g.n(1))
                dve.tensor_reduce(slotf[:, :, :], sel[:, :, :, :], AX_X, ALU.add).then_inc(slotf_ready, 1)
                dve.wait_ge(slotf_ready, g.n(1))
                if g.has(2):
                    dve.wait_ge(scattered[g.par()], g.same(64))
                dve.tensor_copy(slot_now[:, g.par()], slotf[:, :, :]).then_inc(slot_ready, 1)
                dve.tensor_copy(slot_all[:, ds(g.n(0, 2 * T), 2 * T)],
                                slotf[:, :, :].rearrange("p k j -> p (k j)"))

            def tick(u):
                m0, m1, m2, m3, m4 = (u.back(k) for k in range(5))
                if m2.active(NG):
                    capped(m2, 0)
                    maxima(m2, 0)
                if m3.active(NG):
                    low(m3, D3, x2hi_ready, x2s, x2lo_ready)
                if m4.active(NG):
                    choose(m4)
                if m2.active(NG):
                    inverse_sums(m2, 0)
                if m0.active(NG):
                    dve.wait_ge(x_loaded[m0.par()], m0.same_done(8))
                    stats(m0, 0, x_in[:, m0.par()])
                if m1.active(NG):
                    dve.wait_ge(h_done, m1.n(1))
                    dve.tensor_tensor(hb[:, :, :], tiles(D0[:, :]),
                                      rows[:, BC].unsqueeze(1).to_broadcast([P, T, D]), ALU.add)\
                       .then_inc(hb_ready, 1)
                    dve.wait_ge(hb_ready, m1.n(1))
                    stats(m1, 1, hb)
                if m4.active(NG):
                    place(m4)
                if m2.active(NG):
                    capped(m2, 1)
                if m1.active(NG):
                    refine(m1, 1)
                if m2.active(NG):
                    maxima(m2, 1)
                if m1.active(NG):
                    gain(m1, hb, 1, G1)
                    dve.tensor_tensor(hb[:, :, :], hb[:, :, :],
                                      rows[:, BE1].unsqueeze(1).to_broadcast([P, T, D]), ALU.add)\
                       .then_inc(hb_normed, 1)
                    dve.wait_ge(hb_normed, m1.n(1))
                    dve.scalar_tensor_tensor(out=x1[:, m1.par()].rearrange("p a b -> p (a b)"),
                                             in0=hb[:, :, :].rearrange("p a b -> p (a b)"), scalar=0.0,
                                             in1=x0[:, m1.par()].rearrange("p a b -> p (a b)"),
                                             op0=ALU.max, op1=ALU.add).then_inc(x1_ready, 1)
                if m2.active(NG):
                    inverse_sums(m2, 1)
                if m3.active(NG):
                    dve.wait_ge(f2_done, m3.n(1))
                    dve.wait_ge(x2b_ready, m3.n(1))
                    if m3.has(1):
                        dve.wait_ge(r_ready, m3.n())
                    dve.tensor_tensor(zb[:, :, :], tiles(D3[:, :]), x2[:, m3.par()], ALU.add)\
                       .then_inc(zb_ready, 1)
                    dve.wait_ge(zb_ready, m3.n(1))
                    stats(m3, 3, zb)
                if m1.active(NG):
                    low(m1, D0, x1hi_ready, x1s, x1lo_ready)
                if m3.active(NG):
                    refine(m3, 3)
                if m0.active(NG):
                    refine(m0, 0)
                if m3.active(NG):
                    gain(m3, zb, 3, G3)
                    dve.wait_ge(xres_ready, m3.n(1))
                    dve.tensor_tensor(zb[:, :, :], zb[:, :, :], x_res[:, :, :], ALU.add).then_inc(xn_ready, 1)
                    dve.wait_ge(xn_ready, m3.n(1))
                    stats(m3, 4, zb)
                if m2.active(NG):
                    dve.wait_ge(wo_done, m2.n(1))
                    dve.wait_ge(x1b_ready, m2.n(1))
                    dve.tensor_tensor(yb[:, :, :], tiles(D1[:, :]), x1[:, m2.par()], ALU.add)\
                       .then_inc(yb_ready, 1)
                    dve.wait_ge(yb_ready, m2.n(1))
                    stats(m2, 2, yb)
                    refine(m2, 2)
                if m3.active(NG):
                    refine(m3, 4)
                if m2.active(NG):
                    gain(m2, yb, 2, G2)
                    dve.tensor_tensor(x2[:, m2.par()], yb[:, :, :],
                                      rows[:, BE2].unsqueeze(1).to_broadcast([P, T, D]), ALU.add)\
                       .then_inc(x2_ready, 1)

            dve.wait_ge(w_loaded[1], 16 * 11)
            pipeline(dve, NG, 5, tick, 6)

            dve.wait_ge(count_ready, NG)
            base = eighth[:, :]
            link(dve.tensor_scalar(etab[:, 0:E], base, -float(CAP), None, ALU.mult))
            link(dve.tensor_tensor(etab[:, 0:E], etab[:, 0:E], count[:, :], ALU.add))
            link(dve.tensor_scalar(etab_i[:, 0:E], etab[:, 0:E], float(BLK - 1), None, ALU.add))
            link(dve.tensor_scalar(etab_i[:, E:2 * E], etab_i[:, 0:E], BLK.bit_length() - 1, None,
                                   ALU.logical_shift_right))
            link(dve.tensor_copy(etab[:, 0:E], etab_i[:, E:2 * E]))
            link(dve.tensor_copy(etab[:, E:2 * E], etab[:, 0:E]))
            for e in range(1, E):
                link(dve.tensor_tensor(etab[:, E + e:E + e + 1], etab[:, E + e:E + e + 1],
                                       etab[:, E + e - 1:E + e], ALU.add))
            behind = qT[0:1, :, :, :].rearrange("p a b c -> p (a b c)")[:, 0:NBLK * E]\
                .rearrange("p (b e) -> p b e", e=E)
            bi = biota[0:1, :]
            link(dve.tensor_tensor(behind, bi.unsqueeze(2).to_broadcast([1, NBLK, E]),
                                   etab[0:1, E:2 * E].unsqueeze(1).to_broadcast([1, NBLK, E]), ALU.is_ge))
            link(dve.tensor_reduce(brow[0:1, 0, :], behind, AX_X, ALU.add))
            link(dve.tensor_tensor(behind, behind, etab[0:1, 0:E].unsqueeze(1).to_broadcast([1, NBLK, E]),
                                   ALU.mult))
            link(dve.tensor_reduce(brow[0:1, 1, :], behind, AX_X, ALU.add))
            link(dve.tensor_scalar(blk_exp[:, :], brow[0:1, 0, :], float(E - 1), None, ALU.min))
            link(dve.tensor_tensor(brow[0:1, 1, :], bi, brow[0:1, 1, :], ALU.subtract))
            link(dve.tensor_scalar(brow[0:1, 0, :], brow[0:1, 0, :], float(CAP), None, ALU.mult))
            link(dve.scalar_tensor_tensor(out=blk_row[:, :], in0=brow[0:1, 1, :], scalar=float(BLK),
                                          in1=brow[0:1, 0, :], op0=ALU.mult, op1=ALU.add))
            dve.tensor_copy(pad_row[:, :], count[0:1, :]).then_inc(table_ready, 1)
            link(dve.tensor_tensor(etab[:, E:2 * E], etab[:, E:2 * E], etab[:, 0:E], ALU.subtract))
            link(dve.tensor_scalar(etab[:, E:2 * E], etab[:, E:2 * E], float(BLK), None, ALU.mult))
            link(dve.tensor_scalar(etab[:, 0:E], eighth[:, :], float(CAP), None, ALU.mult))
            link(dve.tensor_tensor(etab[:, E:2 * E], etab[:, E:2 * E], etab[:, 0:E], ALU.subtract))
            link(dve.tensor_tensor(etab[:, 1:E], etab[:, E + 1:2 * E], etab[:, E:2 * E - 1], ALU.subtract))
            link(dve.tensor_copy(moved[:, :], slot_all[:, :]))
            for e in range(1, E):
                link(dve.tensor_scalar(shift, slot_all[:, :], float(e * CAP), etab[:, e:e + 1],
                                       ALU.is_ge, ALU.mult))
                link(dve.tensor_tensor(moved, moved, shift, ALU.add))
            link(dve.tensor_copy(slot_all[:, :], moved))
            dve.wait_ge(comb_act, 1)
            link(dve.tensor_scalar(comb[:, 1, :], comb[:, 0, :], 1.0, None, ALU.add))
            link(dve.reciprocal(comb[:, 1, :], comb[:, 1, :]))
            dve.tensor_tensor(comb[:, 2, :], comb[:, 0, :], comb[:, 1, :], ALU.mult).then_inc(comb_ready, 1)
            dve.wait_ge(w_loaded[2], 16 * 6)

            def moe_tick(u):
                b = u.back(1)
                if b.active(NBLK):
                    dve.wait_ge(mt_hi, b.n(1))
                    dve.tensor_tensor(tS[b.par()][:, 1, :, 0:BLK],
                                      D0[:, b.par() * 512:(b.par() + 1) * 512].rearrange("p (c n) -> p c n", c=KC),
                                      tS[b.par()][:, 0, :, 0:BLK], ALU.subtract).then_inc(mt_lo, 1)
                b = u.back(2)
                if b.active(NBLK):
                    h = hid[:, 2 * b.par():2 * b.par() + 2, 0:BLK]
                    dve.wait_ge(mh_gelu, b.n(1))
                    dve.tensor_copy(hS[:, b.par(), 0], h).then_inc(mh_hi, 1)
                    dve.wait_ge(mh_hi, b.n(1))
                    dve.tensor_tensor(hS[:, b.par(), 1], h, hS[:, b.par(), 0], ALU.subtract).then_inc(mh_lo, 1)
                b = u.back(3)
                if b.active(NBLK):
                    e = dve.value_load(blk_exp[0:1, ds(b.n(), 1)], min_val=0, max_val=E - 1)
                    dve.wait_ge(m2_done, b.n(1))
                    if b.has(2):
                        dve.wait_ge(y_stored[b.par()], b.same(8))
                    for j in range(TB):
                        last = dve.scalar_tensor_tensor(
                            out=x2[:, b.par(), j], in0=D2[:, b.par() * 512 + j * D:b.par() * 512 + (j + 1) * D],
                            scalar=1 / WS, in1=m_b2[:, ds(e * D, D)], op0=ALU.mult, op1=ALU.add)
                    last.then_inc(y_ready, 1)

            pipeline(dve, NBLK, 5, moe_tick, 6)

            def mix_tick(u):
                g = u
                if g.active(NG):
                    if g.has(2):
                        dve.wait_ge(gathered[g.par()], g.same(64))
                    dve.tensor_copy(idx2[:, g.par()].rearrange("p k j -> p (k j)"),
                                    slot_all[:, ds(g.n(0, 2 * T), 2 * T)]).then_inc(idx_ready, 1)
                g = u.back(1)
                if g.active(NG):
                    par = g.par()
                    dve.wait_ge(gathered[par], g.same_done(64))
                    dve.wait_ge(rl_loaded[par], g.same_done(8))
                    if g.has(2):
                        dve.wait_ge(out_stored[par], g.same(8))
                    for j in range(T):
                        last = dve.scalar_tensor_tensor(
                            out=x0[:, par, j], in0=x1[:, par, j], scalar=comb[:, 1, ds(g.n(0, T) + j, 1)],
                            in1=x_in[:, par, j], op0=ALU.mult, op1=ALU.add)
                    last.then_inc(mix1, 1)
                    dve.wait_ge(mix1, g.n(1))
                    for j in range(T):
                        last = dve.scalar_tensor_tensor(
                            out=x0[:, par, j], in0=x2[:, par, j], scalar=comb[:, 2, ds(g.n(0, T) + j, 1)],
                            in1=x0[:, par, j], op0=ALU.mult, op1=ALU.add)
                    last.then_inc(mix2, 1)

            pipeline(dve, NG, 2, mix_tick, 4)

        @block.tensor
        def _(pe):
            dve_n = [0]

            def dve_step():
                dve_n[0] += 1
                pe.wait_ge(eig_dve, dve_n[0])

            pe.wait_ge(const_ready, 1)
            pe.wait_ge(w_loaded[0], 16)
            pe.transpose(D3[:, 0:P], A[:, :], ident[:, :]).then_inc(eig_pe, 1)
            dve_step()
            pe.wait_ge(eig_act, 1)
            pe.transpose(D3[0:1, P:2 * P], tiny[:, 0:1], ident[:, :]).then_inc(eig_pe, 1)
            dve_step()
            pe.matmul(D3[:, 256:257], ones[0:1, :], tiny[0:1, 2:3], start=True, stop=True).then_inc(eig_pe, 1)
            dve_step()
            for i in range(SQUARINGS):
                s = sq[:, i % 2]
                pe.matmul(D2[:, (i % 2) * 512:(i % 2) * 512 + P], s, s, start=True, stop=True).then_inc(eig_pe, 1)
                dve_step()
                if i % NORM_EVERY == NORM_EVERY - 1:
                    pe.matmul(D3[:, 256:257], ones[:, :], tiny[:, 5:6], start=True, stop=True)\
                      .then_inc(eig_pe, 1)
                    dve_step()
            dve_step()
            pe.matmul(D3[:, 256:258], ones[:, :], tiny[:, 8:10], start=True, stop=True).then_inc(eig_pe, 1)

            def transposed(src, bank):
                for c in range(KC):
                    for j in range(T):
                        last = pe.transpose(bank[:, c * GT + j * P:c * GT + (j + 1) * P],
                                            src[:, j, c * P:(c + 1) * P], ident[:, :])
                return last

            def project(bank, lhs, w, chunks):
                for j in range(T):
                    for c in range(chunks):
                        last = pe.matmul(bank[:, j * D:(j + 1) * D], lhs[:, c, j * P:(j + 1) * P], w[:, c],
                                         start=(c == 0), stop=(c == chunks - 1))
                return last

            def split_cols(bank, w, col, parts):
                for m in range(2):
                    n = 0
                    for a, b in PARTS:
                        for c in range(KC):
                            last = pe.matmul(bank[:, m * GT:(m + 1) * GT],
                                             w[:, a, c, col + m * P:col + (m + 1) * P], parts[:, b, c],
                                             start=(n == 0), stop=(n == len(PARTS) * KC - 1))
                            n += 1
                return last

            def split_rows(bank, w, parts):
                for j in range(T):
                    n = 0
                    for a, b in PARTS:
                        for c in range(KC):
                            last = pe.matmul(bank[:, j * D:(j + 1) * D], parts[:, b, c, j * P:(j + 1) * P],
                                             w[:, a, c], start=(n == 0), stop=(n == len(PARTS) * KC - 1))
                            n += 1
                return last

            def scores(g, jj):
                if jj == 0:
                    if g.has(1):
                        pe.wait_ge(yb_ready, g.n())
                    pe.wait_ge(q_ready, g.n(1))
                    pe.wait_ge(k_ready, g.n(1))
                else:
                    pe.wait_ge(sc_capped[0], g.n(1))
                q, k = qT[:, g.par()], kT[:, g.par()]
                for j in range(2):
                    tok = slice((2 * jj + j) * P, (2 * jj + j + 1) * P)
                    for m in range(KC):
                        for r in range(2):
                            col = (r * 4 + j * 2 + m) * P
                            last = pe.matmul(D1[:, col:col + P], q[r * HD:(r + 1) * HD, m, tok],
                                             k[r * HD:(r + 1) * HD, m, tok], start=True, stop=True)
                last.then_inc(sc_done[jj], 1)

            def turn_probs(g, jj):
                pe.wait_ge(prob_ready[jj], g.n(1))
                if jj == 0:
                    if g.has(2):
                        pe.wait_ge(count_ready, g.n(-1))
                else:
                    pe.wait_ge(oT_ready[0], g.n(1))
                for i in range(8):
                    last = pe.transpose(D2[:, i * P:(i + 1) * P], prob[:, jj, i], ident[:, :])
                last.then_inc(pT_done[jj], 1)

            def mix_values(g, jj):
                pe.wait_ge(pT_ready[jj], g.n(1))
                pe.wait_ge(v_ready, g.n(1))
                for j in range(2):
                    for h in range(H):
                        r, m = h % 2, h // 2
                        col = m * 256 + j * P
                        last = pe.matmul(D2[r * HD:(r + 1) * HD, col:col + P],
                                         v[:, g.par(), 2 * jj + j, h * HD:(h + 1) * HD],
                                         pT[:, r * 4 + j * 2 + m], start=True, stop=True)
                last.then_inc(pv_done[jj], 1)

            def tick(u):
                m0, m1, m2, m3, m4 = (u.back(k) for k in range(5))
                if m2.active(NG):
                    scores(m2, 0)
                if m4.active(NG):
                    pe.wait_ge(t_ready, m4.n(1))
                    pe.wait_ge(oT_ready[1], m4.n(2) if m4.reg is not None else min(m4.off + 2, NG))
                    transposed(t_out[:, m4.par()], D2).then_inc(tT_done, 1)
                if m3.active(NG):
                    pe.wait_ge(x2_ready, m3.n(1))
                    if m3.has(1):
                        pe.wait_ge(zb_ready, m3.n())
                    transposed(x2[:, m3.par()], D3).then_inc(x2T_done, 1)
                if m1.active(NG):
                    pe.wait_ge(x0_ready, m1.n(1))
                    if m1.has(1):
                        pe.wait_ge(v_ready, m1.n())
                    for c in range(KC):
                        for j in range(T):
                            last = pe.matmul(D0[:, c * GT + j * P:c * GT + (j + 1) * P],
                                             x0[:, m1.par(), j, c * P:(c + 1) * P], LT[:, :],
                                             start=True, stop=True)
                    last.then_inc(xp_done, 1)
                if m4.active(NG):
                    pe.wait_ge(tT_ready, m4.n(1))
                    for j in range(T):
                        for c in range(KC):
                            last = pe.matmul(D2[:, j * E:(j + 1) * E], tT[:, c, j * P:(j + 1) * P], w_r[:, c],
                                             start=(c == 0), stop=(c == KC - 1))
                    last.then_inc(lg_done, 1)
                if m3.active(NG):
                    pe.wait_ge(x2lo_ready, m3.n(1))
                    split_cols(D3, w_f1, 0, x2s).then_inc(f1_done[0], 1)
                if m1.active(NG):
                    pe.wait_ge(xpT_ready, m1.n(1))
                    project(D0, xpT, w_c, KC).then_inc(h_done, 1)
                if m3.active(NG):
                    pe.wait_ge(hid_ready[0], m3.n(1))
                    split_cols(D3, w_f1, 2 * P, x2s).then_inc(f1_done[1], 1)
                if m4.active(NG):
                    pe.wait_ge(picked_ready, m4.n(1))
                    for j in range(T):
                        for i in range(j + 1):
                            pe.matmul(D2[:, 512 + j * E:512 + (j + 1) * E],
                                      ones_h[:, :] if i < j else before_h[:, :], picked[:, i],
                                      start=(i == 0), stop=(i == j))
                    for i in range(T):
                        last = pe.matmul(D2[:, 512 + T * E:512 + (T + 1) * E], ones_h[:, :], picked[:, i],
                                         start=(i == 0), stop=(i == T - 1))
                    last.then_inc(rank_done, 1)
                if m2.active(NG):
                    scores(m2, 1)
                if m2.active(NG):
                    turn_probs(m2, 0)
                if m3.active(NG):
                    pe.wait_ge(hid_ready[1], m3.n(1))
                    project(D3, hid, w_f2, HC).then_inc(f2_done, 1)
                if m1.active(NG):
                    pe.wait_ge(x1_ready, m1.n(1))
                    transposed(x1[:, m1.par()], D0).then_inc(x1T_done, 1)
                if m2.active(NG):
                    mix_values(m2, 0)
                if m2.active(NG):
                    turn_probs(m2, 1)
                if m2.active(NG):
                    mix_values(m2, 1)
                if m1.active(NG):
                    pe.wait_ge(x1lo_ready, m1.n(1))
                    split_cols(D0, w_qkv[:, 0], 0, x1s).then_inc(q_done, 1)
                if m2.active(NG):
                    pe.wait_ge(oT_ready[1], m2.n(1))
                    pe.wait_ge(sc_capped[1], m2.n(1))
                    project(D1, oT, w_o, KC).then_inc(wo_done, 1)
                if m1.active(NG):
                    pe.wait_ge(q_ready, m1.n(1))
                    split_cols(D0, w_qkv[:, 1], 0, x1s).then_inc(k_done, 1)
                if m1.active(NG):
                    pe.wait_ge(k_ready, m1.n(1))
                    split_rows(D0, w_qkv[:, 2], x1s).then_inc(v_done, 1)

            pe.wait_ge(lt_ready, 1)
            pe.wait_ge(w_loaded[1], 16 * 11)
            pe.wait_ge(w_loaded[2], 16 * 6)
            pe.wait_ge(stage_lo, len(JOBS))
            pipeline(pe, NG, 5, tick, 6)

            pe.wait_ge(table_ready, 1)
            ES = 2 * KC * D

            def moe_tick(u):
                b = u.back(1)
                if b.active(NBLK):
                    pe.wait_ge(mt_loaded[b.par()], b.same_done(8))
                    for c in range(KC):
                        for j in range(TB):
                            last = pe.transpose(D0[:, b.par() * 512 + c * BLK + j * P:
                                                   b.par() * 512 + c * BLK + (j + 1) * P],
                                                t_out[:, b.par(), j, c * P:(c + 1) * P], ident[:, :])
                    last.then_inc(mt_done, 1)
                b = u.back(2)
                if b.active(NBLK):
                    e = pe.value_load(blk_exp[0:1, ds(b.n(), 1)], min_val=0, max_val=E - 1)
                    pe.wait_ge(mt_lo, b.n(1))
                    for m in range(KC):
                        n = 0
                        for a, p in PARTS:
                            for c in range(KC):
                                last = pe.matmul(D1[:, b.par() * 512 + m * BLK:b.par() * 512 + (m + 1) * BLK],
                                                 m_w1[:, ds(e * ES + (a * KC + c) * D + m * P, P)],
                                                 tS[b.par()][:, p, c, 0:BLK],
                                                 start=(n == 0), stop=(n == len(PARTS) * KC - 1))
                                n += 1
                    last.then_inc(m1_done, 1)
                b = u.back(3)
                if b.active(NBLK):
                    e = pe.value_load(blk_exp[0:1, ds(b.n(), 1)], min_val=0, max_val=E - 1)
                    pe.wait_ge(mh_lo, b.n(1))
                    if b.has(2):
                        pe.wait_ge(y_ready, b.n(-1))
                    for j in range(TB):
                        n = 0
                        for a, p in PARTS:
                            for c in range(KC):
                                last = pe.matmul(D2[:, b.par() * 512 + j * D:b.par() * 512 + (j + 1) * D],
                                                 hS[:, b.par(), p, c, j * P:(j + 1) * P],
                                                 m_w2[:, ds(e * ES + (a * KC + c) * D, D)],
                                                 start=(n == 0), stop=(n == len(PARTS) * KC - 1))
                                n += 1
                    last.then_inc(m2_done, 1)

            pipeline(pe, NBLK, 5, moe_tick, 6)


_INS = ['x', 'adj', 'L0_gnn_Wc', 'L0_gnn_bc', 'L0_gnn_g1', 'L0_gnn_be1', 'L0_gnn_Wq', 'L0_gnn_Wk', 'L0_gnn_Wv',
        'L0_gnn_Wo', 'L0_gnn_bo', 'L0_gnn_g2', 'L0_gnn_be2', 'L0_gnn_W1', 'L0_gnn_b1', 'L0_gnn_W2', 'L0_gnn_b2',
        'L0_gnn_g3', 'L0_gnn_be3', 'L0_ffn_router_w', 'L0_ffn_w1', 'L0_ffn_b1', 'L0_ffn_w2', 'L0_ffn_b2']


def kernel(**inputs):
    import numpy as _np
    import concourse.bacc as _bacc
    from concourse import mybir as _mybir
    from concourse.bass_utils import run_bass_kernel_spmd as _run

    nc = _bacc.Bacc("TRN2", target_bir_lowering=False, num_devices=1)
    arrays, args = {}, []
    for name in _INS:
        a = _np.ascontiguousarray(inputs[name])
        arrays[f"in_{name}_dram"] = a
        args.append(nc.dram_tensor(f"in_{name}_dram", a.shape, _mybir.dt.from_np(a.dtype), kind="ExternalInput").ap())
    shape = inputs['x'].shape
    args.append(nc.dram_tensor("out_0_dram", shape, _mybir.dt.float32, kind="ExternalOutput").ap())
    build_program(nc, *args)
    r = _run(nc, [arrays], core_ids=[0])
    return r.results[0]["out_0_dram"]
```

```python
from contextlib import ExitStack

import concourse.bass as bass
import numpy as np
from concourse import mybir

F32 = mybir.dt.float32
F16 = mybir.dt.float16
I32 = mybir.dt.int32
U32 = mybir.dt.uint32
ALU = mybir.AluOpType
ACT = mybir.ActivationFunctionType
AX_X = mybir.AxisListType.X
ds = bass.ds

P = 128
EPS = 1e-5
WS = 64.0
SQUARINGS = 25
NORM_EVERY = 4
KEEP = 3e38
PARTS = ((0, 0), (1, 0), (0, 1))


class Group:

    def __init__(self, eng, off, reg=None, cache=None):
        self.eng, self.off, self.reg = eng, off, reg
        self.cache = {} if cache is None else cache

    def back(self, k):
        return Group(self.eng, self.off - k, self.reg, self.cache)

    def par(self):
        return self.off % 2

    def n(self, k=0, mul=1, plus=0):
        if self.reg is None:
            return (self.off + k) * mul + plus
        key = ((self.off + k) * mul + plus, mul)
        if key not in self.cache:
            self.cache[key] = self.eng.snap(self.reg * mul + key[0])
            self.eng.to_reg(self.cache[key])
        return self.cache[key]

    def same(self, mul=1, mod=2):
        return self.n(-(self.off % mod), mul // mod)

    def same_done(self, mul=1, mod=2):
        return self.n(mod - self.off % mod, mul // mod)

    def has(self, k):
        return self.reg is not None or self.off >= k

    def active(self, stop, start=0):
        return self.reg is not None or start <= self.off < stop


def own_wait(eng, over, semaphore, value):
    eng.wait_ge(over, 1)
    eng.wait_ge(semaphore, value)


def pipeline(eng, count, depth, tick, first, start=0, step=2):
    assert (start + first) % step == 0 and first >= depth - 1
    assert (count - first) % step == 0
    for u in range(start, start + first):
        tick(Group(eng, u))
    with eng.Fori(start + first, start + count - 1, step) as i:
        cache = {}
        for u in range(step):
            tick(Group(eng, u, i, cache))
    for u in range(start + count, start + count + depth - 1):
        tick(Group(eng, u))


def build_program(nc, x, adj, Wc, bc, g1, be1, Wq, Wk, Wv, Wo, bo, g2, be2, W1, b1, W2, b2, g3, be3,
                  router_w, mw1, mb1, mw2, mb2, out):
    NB, N, D = x.shape
    H = 4
    HD = D // H
    HID = W1.shape[1]
    E = router_w.shape[0]
    TOK = NB * N
    KC = D // P
    HC = HID // P
    T = 4
    NG = NB // T
    GT = T * P
    assert N == P and KC == 2 and H == 4 and HD == 64 and T == 4
    BLK = 256
    TB = BLK // P
    PAIR = TOK + 2 * BLK
    DUMMY = E // 2 * PAIR
    ROWS = DUMMY + E * BLK
    NBLK = TOK // BLK + E
    ID, W2C, NEXT, W1C, RES = D, D + 1, D + 2, D + 3, D + 4
    ROW2, ROW1 = NEXT, RES + D
    assert ROWS < 1 << 24 and ROWS * ROW1 * 4 < 1 << 31
    HALVES = (slice(0, T // 2), slice(T // 2, T))
    MASKED = -1e9 * float(np.sqrt(HD))

    ctx = ExitStack()
    with ctx:
        def sb(name, shape, dt=F32):
            return ctx.enter_context(nc.sbuf_tensor(name, shape, dt))

        def sem(name):
            return ctx.enter_context(nc.semaphore(name))

        slots = [nc.dram_tensor(f"choice{k}_rows", [ROWS, (ROW1, ROW2)[k]], F32, kind="Internal").ap()
                 for k in range(2)]
        partial = nc.dram_tensor("partial_sums", [ROWS, D], F32, kind="Internal").ap()

        ident = sb("ident", [P, P])
        ones = sb("ones", [P, P])
        ones_h = sb("ones_h", [P, P], F16)
        before_h = sb("before_h", [P, P], F16)
        eighth = sb("eighth", [P, E])
        blank = sb("blank", [P, ROW1])
        w_c = sb("w_c", [P, 2, KC, D], F16)
        w_o = sb("w_o", [P, KC, D])
        w_qkv = sb("w_qkv", [P, 3, 2, KC, D], F16)
        w_f1 = sb("w_f1", [P, 2, KC, HID], F16)
        w_f2 = sb("w_f2", [P, HC, D])
        w_r = sb("w_r", [P, KC, E])
        m_w1 = sb("m_w1", [P, E * 2 * KC * D], F16)
        m_w2 = sb("m_w2", [P, E * 2 * KC * D], F16)
        m_b1 = sb("m_b1", [P, E * KC])
        m_b2 = sb("m_b2", [P, E * D])
        f_b1 = sb("f_b1", [P, HC])
        rows = sb("rows", [P, 9, D])
        BC, G1, BE1, BO, G2, BE2, B2, G3, BE3 = range(9)
        EXP_LN = 6
        A = sb("A", [P, P])
        AT = sb("AT", [P, P])
        LT = sb("LT", [P, P])
        cap = sb("cap", [P, P])

        x_in = sb("x_in", [P, 2, T, D])
        x0 = sb("x0", [P, 2, T, D])
        xps = sb("xps", [P, 2, KC, GT], F16)
        hb = sb("hb", [P, T, D])
        x1 = sb("x1", [P, 2, T, D])
        x1s = sb("x1s", [P, 2, KC, GT], F16)
        qT = sb("qT", [P, KC, GT])
        kT = sb("kT", [P, KC, GT])
        v = sb("v", [P, 2, T, D])
        prob = sb("prob", [P, 2, 8, P])
        pT = sb("pT", [P, 8, P])
        oT = sb("oT", [P, KC, GT])
        yb = sb("yb", [P, T, D])
        x2 = sb("x2", [P, 2, T, D])
        x2s = sb("x2s", [P, 2, KC, GT], F16)
        hid = sb("hid", [P, HC, GT])
        zb = sb("zb", [P, T, D])
        x_res = sb("x_res", [P, T, D])
        row_out = sb("row_out", [P, 2, T, ROW1])
        tT = sb("tT", [P, KC, GT])
        st = sb("st", [P, 5, T, 6])
        mv = sb("mv", [P, 5, T, 2])
        lnv = sb("lnv", [P, 5, T])
        root0 = sb("root0", [P, 5, T])
        eps = sb("eps", [P, 1])
        nh = sb("nh", [P, 5, T])
        nt = sb("nt", [P, 5, T])
        shifts = sb("shifts", [P, 5, T])
        rstd = sb("rstd", [P, 5, T])
        mx = sb("mx", [P, 2, 8])
        nmx = sb("nmx", [P, 2, 8])
        rsum = sb("rsum", [P, 2, 8])
        rinv = sb("rinv", [P, 2, 8])
        lg = sb("lg", [P, T, E])
        top = sb("top", [P, T, 8])
        topi = sb("topi", [P, T, 8], U32)
        topf = sb("topf", [P, 2, T])
        oneh = sb("oneh", [P, T, 2, E])
        picked = sb("picked", [P, T, 2, E], F16)
        pos = sb("pos", [P, T, 2, E])
        sel = sb("sel", [P, T, 2, E])
        slotf = sb("slotf", [P, T, 2])
        slot_now = sb("slot_now", [P, 2, 2, T], U32)
        sign = sb("sign", [P, E])
        start = sb("start", [P, 2, E])
        below = sb("below", [P, 2, E])
        count = sb("count", [P, 2, E])
        d_top = sb("d_top", [P, T])
        e_top = sb("e_top", [P, T])
        idx = sb("idx", [P, 8, TB], U32)
        biota = sb("biota", [P, NBLK])
        brow = yb[0:1, 0:2, 0:2 * NBLK].rearrange("o i (k b) -> o i k b", k=2)
        behind = hid[0:1, :, :].rearrange("p a b -> p (a b)")[:, 0:2 * NBLK * E]\
            .rearrange("p (k b e) -> p k b e", k=2, e=E)
        hS = sb("hS", [P, 2, 2, KC, BLK], F16)
        tiny = sb("tiny", [P, 16])
        etab = sb("etab", [P, 2, 2, E])
        etab_i = sb("etab_i", [P, 2, 2, E], I32)
        blk_row = sb("blk_row", [1, 2 * NBLK + 8], I32)
        blk_exp = sb("blk_exp", [1, 2 * NBLK + 8], I32)
        pad_row = sb("pad_row", [1, 2 * E], I32)
        blk_row_w, blk_exp_w = blk_row[:, 0:2 * NBLK], blk_exp[:, 0:2 * NBLK]
        row_in = [row_out[:, i // 2, (i % 2) * TB:(i % 2 + 1) * TB] for i in range(4)]
        for t in (x_in, x0, x1, v):
            row_in.append(t[:, :, :, :].rearrange("p a j f -> p (a j f)")[:, 0:TB * ROW1]
                          .rearrange("p (j f) -> p j f", j=TB))
        NROW = len(row_in)
        y_out = [x2[:, i // 2, (i % 2) * TB:(i % 2 + 1) * TB] for i in range(4)]
        NY = len(y_out)

        D0 = ctx.enter_context(nc.psum_tensor("D0", [P, 1024], F32))
        D1 = ctx.enter_context(nc.psum_tensor("D1", [P, 1024], F32))
        D2 = ctx.enter_context(nc.psum_tensor("D2", [P, 1024], F32))
        D3 = ctx.enter_context(nc.psum_tensor("D3", [P, 1024], F32))

        stage = hid[:, :, :].rearrange("p a b -> p (a b)")
        S2 = hb[:, 0, 0:P]
        sabs = hb[:, 0, P:2 * P]
        sq = hb[:, 1, :].rearrange("p (i n) -> p i n", i=2)
        tS = (x1s, x2s)
        EIG_DVE = 3 + SQUARINGS + SQUARINGS // NORM_EVERY

        w_loaded = [sem(f"w_loaded{i}") for i in range(3)]
        stage_loaded = [sem(f"stage_loaded{i}") for i in range(2)]
        stage_hi = sem("stage_hi")
        stage_lo = sem("stage_lo")
        const_ready = sem("const_ready")
        eig_pe = sem("eig_pe")
        eig_dve = sem("eig_dve")
        eig_act = sem("eig_act")
        lt_ready = sem("lt_ready")
        pad_zeroed = sem("pad_zeroed")
        x_loaded = [sem(f"x_loaded{i}") for i in range(2)]
        stats_step = [sem(f"stats_step{i}") for i in range(5)]
        root_step = [sem(f"root_step{i}") for i in range(5)]
        refine_step = [sem(f"refine_step{i}") for i in range(5)]
        white_ready = {i: sem(f"white_ready{i}") for i in (1, 2, 3)}
        gained = {i: sem(f"gained{i}") for i in (1, 2, 3)}
        filled = sem("filled")
        x0_ready = sem("x0_ready")
        xp_done = sem("xp_done")
        xphi_ready = sem("xphi_ready")
        xplo_ready = sem("xplo_ready")
        h_done = sem("h_done")
        hb_ready = sem("hb_ready")
        hb_normed = sem("hb_normed")
        x1_ready = sem("x1_ready")
        x1T_done = sem("x1T_done")
        x1hi_ready = sem("x1hi_ready")
        x1lo_ready = sem("x1lo_ready")
        q_done = sem("q_done")
        q_ready = sem("q_ready")
        k_done = sem("k_done")
        k_ready = sem("k_ready")
        v_done = sem("v_done")
        v_ready = sem("v_ready")
        x1b_ready = sem("x1b_ready")
        sc_done = [sem(f"sc_done{i}") for i in range(2)]
        sc_capped = [sem(f"sc_capped{i}") for i in range(2)]
        mx_ready = [sem(f"mx_ready{i}") for i in range(2)]
        nmx_ready = [sem(f"nmx_ready{i}") for i in range(2)]
        exp_done = [sem(f"exp_done{i}") for i in range(2)]
        rinv_ready = [sem(f"rinv_ready{i}") for i in range(2)]
        prob_ready = [sem(f"prob_ready{i}") for i in range(2)]
        pT_done = [sem(f"pT_done{i}") for i in range(2)]
        pT_ready = [sem(f"pT_ready{i}") for i in range(2)]
        pv_done = [sem(f"pv_done{i}") for i in range(2)]
        oT_ready = [sem(f"oT_ready{i}") for i in range(2)]
        wo_done = sem("wo_done")
        yb_ready = sem("yb_ready")
        x2_ready = sem("x2_ready")
        x2T_done = sem("x2T_done")
        x2b_ready = sem("x2b_ready")
        x2hi_ready = sem("x2hi_ready")
        x2lo_ready = sem("x2lo_ready")
        f1_done = [sem(f"f1_done{i}") for i in range(2)]
        hid_ready = [sem(f"hid_ready{i}") for i in range(2)]
        f2_done = sem("f2_done")
        zb_ready = sem("zb_ready")
        xres_loaded = sem("xres_loaded")
        xres_ready = sem("xres_ready")
        xn_ready = sem("xn_ready")
        t_ready = sem("t_ready")
        r_ready = sem("r_ready")
        tT_done = sem("tT_done")
        tT_ready = sem("tT_ready")
        lg_done = sem("lg_done")
        lg_ready = sem("lg_ready")
        top_ready = sem("top_ready")
        topi_ready = sem("topi_ready")
        topf_ready = sem("topf_ready")
        oneh_ready = sem("oneh_ready")
        picked_ready = sem("picked_ready")
        rank_done = sem("rank_done")
        pos_ready = sem("pos_ready")
        sel_ready = sem("sel_ready")
        slotf_ready = sem("slotf_ready")
        slot_ready = sem("slot_ready")
        count_ready = sem("count_ready")
        scattered = [sem(f"scattered{i}") for i in range(2)]
        table_step = sem("table_step")
        table_ready = sem("table_ready")
        d_ready = sem("d_ready")
        e_ready = sem("e_ready")
        weight_step = sem("weight_step")
        weights_ready = sem("weights_ready")
        mt_loaded = [sem(f"mt_loaded{i}") for i in range(NROW)]
        idx_ready = sem("idx_ready")
        y_scaled = sem("y_scaled")
        y_scattered = [sem(f"y_scattered{i}") for i in range(NY)]
        partial_loaded = [sem(f"partial_loaded{i}") for i in range(NROW)]
        mt_done = sem("mt_done")
        mt_hi = sem("mt_hi")
        mt_lo = sem("mt_lo")
        m1_done = sem("m1_done")
        mh_gelu = sem("mh_gelu")
        mh_hi = sem("mh_hi")
        mh_lo = sem("mh_lo")
        m2_done = sem("m2_done")
        y_ready = sem("y_ready")

        x_v = x.rearrange("b n f -> n b f")
        out_rows = out.rearrange("b n f -> (b n) f")
        mw1_v = mw1.rearrange("e (c p) n -> p e c n", p=P)
        mw2_v = mw2.rearrange("e (c p) n -> p e c n", p=P)

        def split_jobs():
            jobs = [(Wc.rearrange("(c p) n -> p c n", p=P), [P, KC, D], w_c[:, 0], w_c[:, 1])]
            for i, w in enumerate((Wq, Wk, Wv)):
                jobs.append((w.rearrange("(c p) n -> p c n", p=P), [P, KC, D],
                             w_qkv[:, i, 0], w_qkv[:, i, 1]))
            jobs.append((W1.rearrange("(c p) n -> p c n", p=P), [P, KC, HID], w_f1[:, 0], w_f1[:, 1]))
            for src, dst in ((mw1_v, m_w1), (mw2_v, m_w2)):
                d = dst[:, :].rearrange("p (e s c n) -> p e s c n", e=E, s=2, c=KC)
                for e in range(0, E, 2):
                    jobs.append((src[:, e:e + 2], [P, 2, KC, D], d[:, e:e + 2, 0], d[:, e:e + 2, 1]))
            return jobs

        JOBS = split_jobs()

        def staged(n):
            shape = JOBS[n][1]
            cols = int(np.prod(shape[1:]))
            flat = stage[:, (n % 2) * 1024:(n % 2) * 1024 + cols]
            if len(shape) == 3:
                return flat.rearrange("p (a b) -> p a b", a=shape[1])
            return flat.rearrange("p (a b c) -> p a b c", a=shape[1], b=shape[2])

        block = ctx.enter_context(nc.Block())

        @block.sync
        def _(sp):
            sp.dma_start(A[:, :], adj).then_inc(w_loaded[0], 16)
            for i, r in enumerate((bc, g1, be1, bo, g2, be2, b2, g3, be3)):
                sp.dma_start(rows[:, i, :], r.partition_broadcast(P)).then_inc(w_loaded[1], 16)
            sp.dma_start(f_b1[:, :], b1.rearrange("(c p) -> p c", p=P), allow_slow_non_contiguous=True).then_inc(w_loaded[1], 16)
            for n, (src, _, _, _) in enumerate(JOBS):
                if n >= 2:
                    sp.wait_ge(stage_lo, n - 1)
                sp.dma_start(staged(n), src).then_inc(stage_loaded[n % 2], 16)
            sp.dma_start(w_o[:, :, :], Wo.rearrange("(c p) n -> p c n", p=P)).then_inc(w_loaded[2], 16)
            sp.dma_start(w_f2[:, :, :], W2.rearrange("(c p) n -> p c n", p=P)).then_inc(w_loaded[2], 16)
            for c in range(KC):
                sp.dma_start(w_r[:, c, :], router_w[:, c * P:(c + 1) * P].rearrange("e p -> p e"), allow_slow_non_contiguous=True)\
                  .then_inc(w_loaded[2], 16)
            sp.dma_start(m_b1[:, :], mb1.rearrange("e (c p) -> p (e c)", p=P), allow_slow_non_contiguous=True).then_inc(w_loaded[2], 16)
            sp.dma_start(m_b2[:, :], mb2.rearrange("e n -> (e n)").partition_broadcast(P))\
              .then_inc(w_loaded[2], 16)
            sp.wait_ge(const_ready, 1)
            for rows_of in (*slots, partial):
                for i in range((ROWS - DUMMY) // P):
                    row = DUMMY + i * P
                    sp.dma_start(rows_of[row:row + P, :], blank[:, 0:rows_of.shape[1]]).then_inc(pad_zeroed, 16)

            def tick(u):
                g = u
                if g.active(NG):
                    if g.has(2):
                        sp.wait_ge(x0_ready, g.n(-1))
                    sp.dma_start(x_in[:, g.par()], x_v[:, ds(g.n(0, T), T), :])\
                      .then_inc(x_loaded[g.par()], 16)
                g = u.back(3)
                if g.active(NG):
                    if g.has(1):
                        sp.wait_ge(xn_ready, g.n(0, 2))
                    sp.dma_start(x_res[:, :, :], x_v[:, ds(g.n(0, T), T), :]).then_inc(xres_loaded, 16)

            pipeline(sp, NG, 5, tick, 6)

            sp.wait_ge(scattered[0], 16 * T * NG)
            sp.wait_ge(scattered[1], 16 * T * NG)
            sp.wait_ge(table_ready, 1)
            zeroed = 3 * ((ROWS - DUMMY) // P)
            for k in range(2):
                targets = ((slots[0],), (slots[1], partial))[k]
                for e in range(E):
                    row = sp.value_load(pad_row[0:1, k * E + e:k * E + e + 1], min_val=e // 2 * PAIR,
                                        max_val=e // 2 * PAIR + PAIR - BLK)
                    for rows_of in targets:
                        width = rows_of.shape[1]
                        sp.dma_start(rows_of[ds(row, BLK), :].rearrange("(b p) f -> p b f", p=P),
                                     blank[:, 0:width].unsqueeze(1).to_broadcast([P, TB, width]))\
                          .then_inc(pad_zeroed, 16)
                zeroed += E * len(targets)
                sp.wait_ge(pad_zeroed, 16 * zeroed)
                if k == 1:
                    for i in range(NY):
                        sp.wait_ge(y_scattered[i], 16 * TB * NBLK // NY)

                def moe_tick(u):
                    b = u
                    if b.active((k + 1) * NBLK, k * NBLK):
                        if b.has(NROW):
                            sp.wait_ge(y_ready, b.n(1 - NROW))
                        row = sp.value_load(blk_row[0:1, ds(b.n(), 1)], min_val=0, max_val=ROWS - BLK)
                        cols = slots[k].shape[1]
                        sp.dma_start(row_in[b.off % NROW][:, :, 0:cols],
                                     slots[k][ds(row, BLK), :].rearrange("(b p) f -> p b f", p=P))\
                          .then_inc(mt_loaded[b.off % NROW], 16)
                        if k == 1:
                            sp.dma_start(row_in[b.off % NROW][:, :, RES:ROW1],
                                         partial[ds(row, BLK), :].rearrange("(b p) f -> p b f", p=P))\
                              .then_inc(partial_loaded[b.off % NROW], 16)

                pipeline(sp, NBLK, 6, moe_tick, 8, start=k * NBLK, step=NROW)

        @block.gpsimd
        def _(pool):
            pool.memset(blank[:, :], 0.0)
            pool.memset(ones[:, :], 1.0)
            pool.memset(ones_h[:, :], 1.0)
            pool.memset(before_h[:, :], 1.0)
            pool.memset(ident[:, :], 0.0)
            pool.memset(eps[:, :], EPS)
            pool.iota(eighth[:, :], [[1, E]], base=0, channel_multiplier=0,
                      allow_small_or_imprecise_dtypes=True)
            pool.iota(biota[:, :], [[1, NBLK]], base=0, channel_multiplier=0,
                      allow_small_or_imprecise_dtypes=True)
            for par in range(2):
                pool.iota(row_out[:, par, :, ID], [[P, T]], base=(par - 2) * GT, channel_multiplier=1,
                          allow_small_or_imprecise_dtypes=True)
            pool.iota(sign[:, :], [[0, E // 2], [-2, 2]], base=1, channel_multiplier=0,
                      allow_small_or_imprecise_dtypes=True)
            pool.iota(below[:, :, :], [[0, 2], [0, E // 2], [1 - BLK, 2]], base=0, channel_multiplier=0,
                      allow_small_or_imprecise_dtypes=True)
            pool.iota(start[:, :, :], [[0, 2], [PAIR, E // 2], [PAIR - 1, 2]], base=0, channel_multiplier=0,
                      allow_small_or_imprecise_dtypes=True)
            pool.iota(count[:, :, :], [[0, 2], [PAIR, E // 2], [PAIR - 1, 2]], base=0, channel_multiplier=0,
                      allow_small_or_imprecise_dtypes=True).then_inc(filled, 1)
            pool.wait_ge(filled, 1)
            pool.memset(blank[:, ID:ID + 1], float(ROWS))
            pool.memset(blank[:, NEXT:NEXT + 1], float(ROWS))
            pool.affine_select(out=before_h[:, :], in_=before_h[:, :], compare_op=ALU.is_gt, fill=0.0,
                               base=0, pattern=[[1, P]], channel_multiplier=-1)
            pool.affine_select(out=ident[:, :], in_=ident[:, :], compare_op=ALU.not_equal, fill=1.0,
                               base=0, pattern=[[-1, P]], channel_multiplier=1).then_inc(const_ready, 1)

            def add_row(dst, i):
                return pool.tensor_tensor(dst, dst, rows[:, i].unsqueeze(1).to_broadcast([P, T, D]), ALU.add)

            def normalise(g, jj):
                pool.wait_ge(rinv_ready[jj], g.n(1))
                pool.tensor_tensor(prob[:, jj], prob[:, jj],
                                   rinv[:, jj].unsqueeze(2).to_broadcast([P, 8, P]), ALU.mult)\
                    .then_inc(prob_ready[jj], 1)

            def tick(u):
                m0, m1, m2, m3, m4 = (u.back(k) for k in range(5))
                if m2.active(NG):
                    pool.wait_ge(x1T_done, m2.n(1))
                    add_row(x1[:, m2.par()], BO).then_inc(x1b_ready, 1)
                if m3.active(NG):
                    pool.wait_ge(x2T_done, m3.n(1))
                    add_row(x2[:, m3.par()], B2).then_inc(x2b_ready, 1)
                if m2.active(NG):
                    normalise(m2, 0)
                    normalise(m2, 1)
                if m3.active(NG):
                    pool.wait_ge(xres_loaded, m3.n(1, 16))
                    add_row(x_res[:, :, :], BE3).then_inc(xres_ready, 1)
                if m4.active(NG):
                    own_wait(pool, const_ready, slot_ready, m4.n(1))
                    pool.wait_ge(r_ready, m4.n(1))
                    pool.wait_ge(weights_ready, m4.n(1))
                    for j in range(T):
                        for k in range(2):
                            pool.indirect_dma_start(
                                out=slots[k], in_=row_out[:, m4.par(), j, 0:slots[k].shape[1]], in_offset=None,
                                out_offset=bass.IndirectOffsetOnAxis(ap=slot_now[:, m4.par(), k, j:j + 1],
                                                                     axis=0))\
                                .then_inc(scattered[m4.par()], 16)
                if m3.active(NG):
                    pool.wait_ge(t_ready, m3.n(1))
                    pool.tensor_tensor(row_out[:, m3.par(), :, RES:ROW1], zb[:, :, :],
                                       row_out[:, m3.par(), :, 0:D], ALU.add).then_inc(r_ready, 1)

            pool.wait_ge(w_loaded[1], 16 * 10)
            pipeline(pool, NG, 5, tick, 6)

            for k in range(2):
                def moe_tick(u):
                    lo, hi = k * NBLK, (k + 1) * NBLK
                    b = u.back(4)
                    if b.active(hi, lo):
                        own_wait(pool, const_ready, y_ready, b.n(1))
                        for j in range(TB):
                            pool.indirect_dma_start(
                                out=(partial, out_rows)[k], in_=y_out[b.off % NY][:, j, :], in_offset=None,
                                out_offset=bass.IndirectOffsetOnAxis(ap=idx[:, b.off % NROW, j:j + 1], axis=0),
                                bounds_check=(ROWS, TOK)[k] - 1, oob_is_err=False).then_inc(y_scattered[b.off % NY], 16)

                pipeline(pool, NBLK, 6, moe_tick, 8, start=k * NBLK, step=NROW)
                for i in range(NY):
                    pool.wait_ge(y_scattered[i], 16 * TB * (k + 1) * NBLK // NY)

        @block.scalar
        def _(act):
            act.wait_ge(eig_dve, 1)
            act.activation(sabs[:, :], S2[:, :], ACT.Abs, accum_out=tiny[:, 0:1]).then_inc(eig_act, 1)
            for n, (_, _, hi, _) in enumerate(JOBS):
                act.wait_ge(stage_loaded[n % 2], 16 * (n // 2 + 1))
                act.activation(hi, staged(n), ACT.Copy, scale=WS).then_inc(stage_hi, 1)

            def flat(t):
                return t.rearrange("p a b -> p (a b)")

            def exps(g, jj):
                act.wait_ge(nmx_ready[jj], g.n(1))
                for i in range(8):
                    last = act.activation(prob[:, jj, i], prob[:, jj, i], ACT.Exp, bias=nmx[:, jj, i:i + 1],
                                          scale=float(1 / np.sqrt(HD)), accum_out=rsum[:, jj, i:i + 1])
                last.then_inc(exp_done[jj], 1)

            def gelus(g, half):
                act.wait_ge(f1_done[half], g.n(1))
                for i in range(2):
                    c = 2 * half + i
                    last = act.activation(hid[:, c], D3[:, i * 512:(i + 1) * 512], ACT.Gelu,
                                          bias=f_b1[:, c:c + 1], scale=1 / WS)
                last.then_inc(hid_ready[half], 1)

            def load_tables(which):
                act.add_instruction(mybir.InstLoadActFuncSet(
                    act_func_set_id=which, name=nc.get_next_instruction_name(), engine=act.engine))

            def root(g, k):
                act.wait_ge(stats_step[k], g.n(1, 3))
                act.activation(lnv[:, k], mv[:, k, :, 1], ACT.Ln, bias=eps[:, :]).then_inc(root_step[k], 1)
                act.wait_ge(root_step[k], g.n(0, 2, 1))
                act.activation(root0[:, k], lnv[:, k], ACT.Exp, scale=-0.5).then_inc(root_step[k], 1)

            def evac_p(g, jj):
                for r in range(2):
                    act.wait_ge(pT_done[jj], g.n(0, 2, r + 1))
                    act.activation(flat(pT[:, r * 4:(r + 1) * 4]), D2[:, r * 512:(r + 1) * 512], ACT.Copy)\
                       .then_inc(pT_ready[jj], 1)

            def evac_o(g, jj):
                act.wait_ge(pv_done[jj], g.n(1))
                act.activation(oT[:, :, jj * 256:(jj + 1) * 256],
                               D2[:, 0:512].rearrange("p (c n) -> p c n", c=KC), ACT.Copy)\
                   .then_inc(oT_ready[jj], 1)

            def evac(g, bank, done, dst, ready, scale):
                act.wait_ge(done, g.n(1))
                act.activation(dst, bank[:, :], ACT.Copy, scale=scale).then_inc(ready, 1)

            def whiten(g, k, dst, src, ready):
                act.wait_ge(refine_step[k], g.n(1, 5))
                for j in range(T):
                    last = act.activation(dst[:, j], src[:, j], ACT.Identity, bias=shifts[:, k, j:j + 1],
                                          scale=rstd[:, k, j:j + 1])
                    if j == T // 2 - 1 and k in white_ready:
                        last.then_inc(ready, 1)
                last.then_inc(ready, 1)

            def tick(u):
                m0, m1, m2, m3, m4 = (u.back(k) for k in range(5))
                if m3.active(NG):
                    evac(m3, D3, x2T_done, flat(x2s[:, 0]), x2hi_ready, 1.0)
                if m4.active(NG):
                    evac(m4, D2, tT_done, flat(tT[:, :, :]), tT_ready, 1.0)
                if m1.active(NG):
                    evac(m1, D0, xp_done, flat(xps[:, 0]), xphi_ready, 1.0)
                if m2.active(NG):
                    exps(m2, 0)
                if m3.active(NG):
                    gelus(m3, 0)
                    gelus(m3, 1)
                    load_tables(EXP_LN)
                if m1.active(NG):
                    root(m1, 1)
                if m2.active(NG):
                    evac_p(m2, 0)
                if m1.active(NG):
                    whiten(m1, 1, hb, hb, white_ready[1])
                if m2.active(NG):
                    exps(m2, 1)
                if m4.active(NG):
                    act.wait_ge(d_ready, m4.n(1))
                    act.activation(e_top[:, :], d_top[:, :], ACT.Exp).then_inc(e_ready, 1)
                if m2.active(NG):
                    evac_o(m2, 0)
                if m0.active(NG):
                    root(m0, 0)
                if m1.active(NG):
                    evac(m1, D0, x1T_done, flat(x1s[:, 0]), x1hi_ready, 1.0)
                if m2.active(NG):
                    evac_p(m2, 1)
                if m3.active(NG):
                    root(m3, 3)
                    whiten(m3, 3, zb, zb, white_ready[3])
                if m2.active(NG):
                    evac_o(m2, 1)
                if m1.active(NG):
                    evac(m1, D0, q_done, flat(qT[:, :, :]), q_ready, 1 / WS)
                if m0.active(NG):
                    whiten(m0, 0, x0[:, m0.par()], x_in[:, m0.par()], x0_ready)
                if m3.active(NG):
                    root(m3, 4)
                if m1.active(NG):
                    evac(m1, D0, k_done, flat(kT[:, :, :]), k_ready, 1 / WS)
                if m2.active(NG):
                    root(m2, 2)
                    whiten(m2, 2, yb, yb, white_ready[2])
                if m3.active(NG):
                    if m3.has(2):
                        act.wait_ge(scattered[m3.par()], m3.same(128))
                    whiten(m3, 4, row_out[:, m3.par(), :, 0:D], zb, t_ready)
                if m1.active(NG):
                    evac(m1, D0, v_done, flat(v[:, m1.par()]), v_ready, 1 / WS)

            load_tables(EXP_LN)
            act.wait_ge(w_loaded[1], 16 * 10)
            pipeline(act, NG, 5, tick, 6)

            act.wait_ge(table_ready, 1)
            act.wait_ge(w_loaded[2], 16 * 6)

            for k in range(2):
                def moe_tick(u):
                    lo, hi = k * NBLK, (k + 1) * NBLK
                    b = u.back(1)
                    if b.active(hi, lo):
                        act.wait_ge(mt_done, b.n(1))
                        act.activation(tS[b.par()][:, 0, :, 0:BLK],
                                       D0[:, b.par() * 512:(b.par() + 1) * 512].rearrange("p (c n) -> p c n", c=KC),
                                       ACT.Copy).then_inc(mt_hi, 1)
                    b = u.back(2)
                    if b.active(hi, lo):
                        e = act.value_load(blk_exp[0:1, ds(b.n(), 1)], min_val=0, max_val=E - 1)
                        act.wait_ge(m1_done, b.n(1))
                        for dst, ready in ((hS[:, b.par(), 0], mh_hi), (hid[:, 2 * b.par():2 * b.par() + 2], mh_gelu)):
                            for m in range(KC):
                                last = act.activation(
                                    dst[:, m, 0:BLK],
                                    D1[:, b.par() * 512 + m * BLK:b.par() * 512 + (m + 1) * BLK],
                                    ACT.Gelu, bias=m_b1[:, ds(e * KC + m, 1)], scale=1 / WS)
                            last.then_inc(ready, 1)

                pipeline(act, NBLK, 6, moe_tick, 8, start=k * NBLK, step=NROW)

        @block.vector
        def _(dve):
            chain = [0]

            def link(ins):
                chain[0] += 1
                ins.then_inc(table_step, 1)
                dve.wait_ge(table_step, chain[0])

            pe_n, jobs = [0], iter(range(len(JOBS)))

            def pe_step():
                pe_n[0] += 1
                dve.wait_ge(eig_pe, pe_n[0])

            def split_lo():
                n = next(jobs, None)
                if n is None:
                    return
                _, _, hi, lo = JOBS[n]
                dve.wait_ge(stage_hi, n + 1)
                s = staged(n)
                if len(s.shape) == 3:
                    dve.scalar_tensor_tensor(out=lo, in0=s, scalar=WS, in1=hi, op0=ALU.mult,
                                             op1=ALU.subtract).then_inc(stage_lo, 1)
                else:
                    for i in range(2):
                        last = dve.scalar_tensor_tensor(out=lo[:, i], in0=s[:, i], scalar=WS, in1=hi[:, i],
                                                        op0=ALU.mult, op1=ALU.subtract)
                    last.then_inc(stage_lo, 1)

            dve.wait_ge(w_loaded[0], 16)
            pe_step()
            link(dve.tensor_copy(AT[:, :], D3[:, 0:P]))
            dve.tensor_tensor(S2[:, :], A[:, :], AT[:, :], ALU.add).then_inc(eig_dve, 1)
            link(dve.tensor_scalar(cap[:, :], A[:, :], 0.0, KEEP, ALU.is_gt, ALU.mult))
            link(dve.tensor_scalar(cap[:, :], cap[:, :], MASKED, None, ALU.add))
            pe_step()
            link(dve.reduce_max(tiny[0:1, 1:2], D3[0:1, P:2 * P], AX_X))
            dve.tensor_scalar(tiny[0:1, 2:3], tiny[0:1, 1:2], 1e-30, None, ALU.max).then_inc(eig_dve, 1)
            pe_step()
            link(dve.tensor_copy(tiny[:, 3:4], D3[:, 256:257]))
            link(dve.reciprocal(tiny[:, 4:5], tiny[:, 3:4]))
            link(dve.scalar_tensor_tensor(out=sq[:, 0], in0=ident[:, :], scalar=tiny[:, 3:4], in1=S2[:, :],
                                          op0=ALU.mult, op1=ALU.add))
            dve.tensor_scalar(sq[:, 0], sq[:, 0], tiny[:, 4:5], 0.5, ALU.mult, ALU.mult).then_inc(eig_dve, 1)
            for i in range(SQUARINGS):
                split_lo()
                pe_step()
                src, dst = D2[:, (i % 2) * 512:(i % 2) * 512 + P], sq[:, (i + 1) % 2]
                if i % NORM_EVERY == NORM_EVERY - 1:
                    dve.tensor_tensor_reduce(sabs[:, :], src, ident[:, :], 1.0, 0.0, ALU.mult, ALU.add,
                                             tiny[:, 5:6]).then_inc(eig_dve, 1)
                    pe_step()
                    link(dve.reciprocal(tiny[:, 6:7], D3[:, 256:257]))
                    dve.tensor_scalar(dst, src, tiny[:, 6:7], None, ALU.mult).then_inc(eig_dve, 1)
                else:
                    dve.tensor_copy(dst, src).then_inc(eig_dve, 1)
            for _ in range(len(JOBS)):
                split_lo()
            last_sq = sq[:, SQUARINGS % 2]
            dve.wait_ge(eig_dve, EIG_DVE)
            link(dve.tensor_tensor_reduce(sabs[:, :], last_sq, S2[:, :], 1.0, 0.0, ALU.mult, ALU.add,
                                          tiny[:, 8:9]))
            dve.tensor_tensor_reduce(sabs[:, :], last_sq, ident[:, :], 1.0, 0.0, ALU.mult, ALU.add,
                                     tiny[:, 9:10]).then_inc(eig_dve, 1)
            pe_step()
            link(dve.tensor_copy(tiny[:, 10:12], D3[:, 256:258]))
            link(dve.reciprocal(tiny[:, 12:13], tiny[:, 11:12]))
            link(dve.scalar_tensor_tensor(out=tiny[:, 13:14], in0=tiny[:, 10:11], scalar=0.5,
                                          in1=tiny[:, 12:13], op0=ALU.mult, op1=ALU.mult))
            link(dve.tensor_scalar(tiny[:, 14:15], tiny[:, 13:14], 1e-8, 0.5, ALU.add, ALU.mult))
            link(dve.reciprocal(tiny[:, 15:16], tiny[:, 14:15]))
            dve.scalar_tensor_tensor(out=LT[:, :], in0=AT[:, :], scalar=tiny[:, 15:16], in1=ident[:, :],
                                     op0=ALU.mult, op1=ALU.subtract).then_inc(lt_ready, 1)

            def stats(g, k, src, halves=None):
                for j in range(T):
                    if halves is not None and j % 2 == 0:
                        dve.wait_ge(halves, g.n(0, 2, j // 2 + 1))
                    last = dve.bn_stats(st[:, k, j], src[:, j])
                    if j % 2 == 1:
                        last.then_inc(stats_step[k], 1)
                for j in range(T):
                    if j % 2 == 0:
                        own_wait(dve, const_ready, stats_step[k], g.n(0, 3, j // 2 + 1))
                    last = dve.bn_aggr(mv[:, k, j], st[:, k, j])
                last.then_inc(stats_step[k], 1)

            def refine(g, k):
                dve.wait_ge(stats_step[k], g.n(1, 3))
                dve.tensor_scalar(nh[:, k], mv[:, k, :, 1], EPS, -0.5, ALU.add, ALU.mult)
                dve.wait_ge(root_step[k], g.n(1, 2))
                dve.tensor_tensor(nt[:, k], root0[:, k], root0[:, k], ALU.mult).then_inc(refine_step[k], 1)
                dve.scalar_tensor_tensor(out=shifts[:, k], in0=mv[:, k, :, 0], scalar=-1.0, in1=root0[:, k],
                                         op0=ALU.mult, op1=ALU.mult).then_inc(refine_step[k], 1)
                dve.wait_ge(refine_step[k], g.n(0, 5, 1))
                dve.tensor_tensor(nt[:, k], nt[:, k], nh[:, k], ALU.mult).then_inc(refine_step[k], 1)
                dve.wait_ge(refine_step[k], g.n(0, 5, 3))
                dve.scalar_tensor_tensor(out=rstd[:, k], in0=nt[:, k], scalar=1.5, in1=root0[:, k],
                                         op0=ALU.add, op1=ALU.mult).then_inc(refine_step[k], 1)
                dve.scalar_tensor_tensor(out=shifts[:, k], in0=nt[:, k], scalar=1.5, in1=shifts[:, k],
                                         op0=ALU.add, op1=ALU.mult).then_inc(refine_step[k], 1)

            def row(i):
                return rows[:, i].unsqueeze(1).to_broadcast([P, T // 2, D])

            def gain(g, buf, k, i):
                for n, half in enumerate(HALVES):
                    dve.wait_ge(white_ready[k], g.n(0, 2, n + 1))
                    dve.tensor_tensor(buf[:, half], buf[:, half], row(i), ALU.mult).then_inc(gained[k], 1)

            def add(g, dst, buf, k, addend, ready):
                for n, half in enumerate(HALVES):
                    dve.wait_ge(gained[k], g.n(0, 2, n + 1))
                    dve.tensor_tensor(dst[:, half], buf[:, half], addend(half), ALU.add).then_inc(ready, 1)

            def tiles(t):
                return t.rearrange("p (j n) -> p j n", j=T)

            def capped(g, jj):
                dve.wait_ge(sc_done[jj], g.n(1))
                dve.tensor_tensor(prob[:, jj], D1[:, :].rearrange("p (a m) -> p a m", m=P),
                                  cap[:, :].unsqueeze(1).to_broadcast([P, 8, P]), ALU.min)\
                   .then_inc(sc_capped[jj], 1)

            def maxima(g, jj):
                dve.wait_ge(sc_capped[jj], g.n(1))
                dve.tensor_reduce(mx[:, jj], prob[:, jj], AX_X, ALU.max).then_inc(mx_ready[jj], 1)
                dve.wait_ge(mx_ready[jj], g.n(1))
                dve.tensor_scalar(nmx[:, jj], mx[:, jj], -float(1 / np.sqrt(HD)), None, ALU.mult)\
                   .then_inc(nmx_ready[jj], 1)

            def inverse_sums(g, jj):
                dve.wait_ge(exp_done[jj], g.n(1))
                dve.reciprocal(rinv[:, jj], rsum[:, jj]).then_inc(rinv_ready[jj], 1)

            def low(g, bank, hi_ready, parts, ready):
                dve.wait_ge(hi_ready, g.n(1))
                dve.tensor_tensor(parts[:, 1].rearrange("p a b -> p (a b)"), bank[:, :],
                                  parts[:, 0].rearrange("p a b -> p (a b)"), ALU.subtract).then_inc(ready, 1)

            def choose(g):
                dve.wait_ge(lg_done, g.n(1))
                dve.tensor_copy(lg[:, :, :], D2[:, 0:T * E].rearrange("p (j e) -> p j e", e=E))\
                   .then_inc(lg_ready, 1)
                own_wait(dve, const_ready, lg_ready, g.n(1))
                for j in range(T):
                    last = dve.max(top[:, j], lg[:, j])
                last.then_inc(top_ready, 1)
                own_wait(dve, const_ready, top_ready, g.n(1))
                for j in range(T):
                    last = dve.max_index(topi[:, j], top[:, j], lg[:, j])
                last.then_inc(topi_ready, 1)
                dve.tensor_tensor(d_top[:, :], top[:, :, 1], top[:, :, 0], ALU.subtract).then_inc(d_ready, 1)
                dve.wait_ge(topi_ready, g.n(1))
                dve.tensor_copy(topf[:, :, :], topi[:, :, 0:2].rearrange("p j k -> p k j"))\
                   .then_inc(topf_ready, 1)
                dve.wait_ge(topf_ready, g.n(1))
                for k in range(2):
                    last = dve.tensor_tensor(oneh[:, :, k], eighth[:, :].unsqueeze(1).to_broadcast([P, T, E]),
                                             topf[:, k].unsqueeze(2).to_broadcast([P, T, E]), ALU.is_equal)
                last.then_inc(oneh_ready, 1)
                dve.wait_ge(oneh_ready, g.n(1))
                for k in range(2):
                    last = dve.tensor_tensor(picked[:, :, k], oneh[:, :, k],
                                             sign[:, :].unsqueeze(1).to_broadcast([P, T, E]), ALU.mult)
                last.then_inc(picked_ready, 1)

            def place(g):
                dve.wait_ge(rank_done, g.n(1))
                dve.tensor_tensor(pos[:, :, :, :].rearrange("p j k e -> p j (k e)"),
                                  D2[:, 512:512 + T * 2 * E].rearrange("p (j e) -> p j e", j=T),
                                  count[:, :, :].rearrange("p k e -> p (k e)").unsqueeze(1)
                                  .to_broadcast([P, T, 2 * E]), ALU.add).then_inc(pos_ready, 1)
                dve.wait_ge(pos_ready, g.n(1))
                dve.tensor_tensor(sel[:, :, :, :], oneh[:, :, :, :], pos[:, :, :, :], ALU.mult).then_inc(sel_ready, 1)
                dve.tensor_tensor(count[:, :, :].rearrange("p k e -> p (k e)"),
                                  count[:, :, :].rearrange("p k e -> p (k e)"),
                                  D2[:, 512 + T * 2 * E:512 + (T + 1) * 2 * E], ALU.add).then_inc(count_ready, 1)
                dve.wait_ge(sel_ready, g.n(1))
                dve.tensor_reduce(slotf[:, :, :], sel[:, :, :, :], AX_X, ALU.add).then_inc(slotf_ready, 1)
                dve.wait_ge(slotf_ready, g.n(1))
                if g.has(2):
                    dve.wait_ge(scattered[g.par()], g.same(128))
                dve.tensor_copy(slot_now[:, g.par()], slotf[:, :, :].rearrange("p j k -> p k j")).then_inc(slot_ready, 1)
                dve.tensor_copy(row_out[:, g.par(), :, NEXT], slotf[:, :, 1])
                number = row_out[:, g.par(), :, ID]
                dve.tensor_scalar(number, number, float(2 * GT), None, ALU.add)

            def weigh(g):
                w1, w2 = row_out[:, g.par(), :, W1C], row_out[:, g.par(), :, W2C]
                dve.wait_ge(e_ready, g.n(1))
                dve.tensor_scalar(w2, e_top[:, :], 1.0, None, ALU.add).then_inc(weight_step, 1)
                dve.wait_ge(weight_step, g.n(0, 2, 1))
                dve.reciprocal(w1, w2).then_inc(weight_step, 1)
                dve.wait_ge(weight_step, g.n(1, 2))
                dve.tensor_tensor(w2, e_top[:, :], w1, ALU.mult).then_inc(weights_ready, 1)

            def tick(u):
                m0, m1, m2, m3, m4 = (u.back(k) for k in range(5))
                if m2.active(NG):
                    capped(m2, 0)
                    maxima(m2, 0)
                if m3.active(NG):
                    low(m3, D3, x2hi_ready, x2s, x2lo_ready)
                if m1.active(NG):
                    low(m1, D0, xphi_ready, xps, xplo_ready)
                if m2.active(NG):
                    inverse_sums(m2, 0)
                if m4.active(NG):
                    choose(m4)
                if m0.active(NG):
                    dve.wait_ge(x_loaded[m0.par()], m0.same_done(16))
                    stats(m0, 0, x_in[:, m0.par()])
                if m1.active(NG):
                    dve.wait_ge(h_done, m1.n(1))
                    for half in HALVES:
                        dve.scalar_tensor_tensor(out=hb[:, half], in0=tiles(D0[:, :])[:, half], scalar=1 / WS,
                                                 in1=row(BC), op0=ALU.mult, op1=ALU.add).then_inc(hb_ready, 1)
                    stats(m1, 1, hb, hb_ready)
                if m4.active(NG):
                    place(m4)
                if m2.active(NG):
                    capped(m2, 1)
                if m1.active(NG):
                    refine(m1, 1)
                if m2.active(NG):
                    maxima(m2, 1)
                if m1.active(NG):
                    gain(m1, hb, 1, G1)
                    add(m1, hb, hb, 1, lambda half: row(BE1), hb_normed)
                    for n, half in enumerate(HALVES):
                        dve.wait_ge(hb_normed, m1.n(0, 2, n + 1))
                        dve.scalar_tensor_tensor(out=x1[:, m1.par(), half], in0=hb[:, half], scalar=0.0,
                                                 in1=x0[:, m1.par(), half], op0=ALU.max, op1=ALU.add)\
                            .then_inc(x1_ready, 1)
                if m2.active(NG):
                    inverse_sums(m2, 1)
                if m3.active(NG):
                    dve.wait_ge(f2_done, m3.n(1))
                    dve.wait_ge(x2b_ready, m3.n(1))
                    if m3.has(1):
                        dve.wait_ge(r_ready, m3.n())
                    for half in HALVES:
                        dve.tensor_tensor(zb[:, half], tiles(D3[:, :])[:, half], x2[:, m3.par(), half], ALU.add)\
                           .then_inc(zb_ready, 1)
                    stats(m3, 3, zb, zb_ready)
                if m1.active(NG):
                    low(m1, D0, x1hi_ready, x1s, x1lo_ready)
                if m3.active(NG):
                    refine(m3, 3)
                if m0.active(NG):
                    refine(m0, 0)
                if m3.active(NG):
                    gain(m3, zb, 3, G3)
                    dve.wait_ge(xres_ready, m3.n(1))
                    add(m3, zb, zb, 3, lambda half: x_res[:, half], xn_ready)
                    stats(m3, 4, zb, xn_ready)
                if m2.active(NG):
                    dve.wait_ge(wo_done, m2.n(1))
                    dve.wait_ge(x1b_ready, m2.n(1))
                    for half in HALVES:
                        dve.tensor_tensor(yb[:, half], tiles(D1[:, :])[:, half], x1[:, m2.par(), half], ALU.add)\
                           .then_inc(yb_ready, 1)
                    stats(m2, 2, yb, yb_ready)
                if m4.active(NG):
                    weigh(m4)
                if m2.active(NG):
                    refine(m2, 2)
                if m3.active(NG):
                    refine(m3, 4)
                if m2.active(NG):
                    gain(m2, yb, 2, G2)
                    add(m2, x2[:, m2.par()], yb, 2, lambda half: row(BE2), x2_ready)

            dve.wait_ge(w_loaded[1], 16 * 10)
            pipeline(dve, NG, 5, tick, 6)

            dve.wait_ge(count_ready, NG)
            blocks, ends = etab[:, 0], etab[:, 1]
            link(dve.tensor_tensor(ends, count[:, :, :], start[:, :, :], ALU.subtract))
            for k in range(2):
                link(dve.tensor_tensor(blocks[:, k], ends[:, k], sign[:, :], ALU.mult))
            link(dve.tensor_tensor(start[:, :, :], count[:, :, :], below[:, :, :], ALU.add))
            link(dve.tensor_scalar(etab_i[:, 0], blocks, float(BLK - 1), None, ALU.add))
            link(dve.tensor_scalar(etab_i[:, 1], etab_i[:, 0], BLK.bit_length() - 1, None,
                                   ALU.logical_shift_right))
            link(dve.tensor_copy(blocks, etab_i[:, 1]))
            link(dve.tensor_copy(ends, blocks))
            for e in range(1, E):
                link(dve.tensor_tensor(ends[:, :, e:e + 1], ends[:, :, e:e + 1], ends[:, :, e - 1:e], ALU.add))
            bi = biota[0:1, :].unsqueeze(1).to_broadcast([1, 2, NBLK])
            for k in range(2):
                link(dve.tensor_tensor(behind[:, k], biota[0:1, :].unsqueeze(2).to_broadcast([1, NBLK, E]),
                                       ends[0:1, k].unsqueeze(1).to_broadcast([1, NBLK, E]), ALU.is_ge))
            link(dve.tensor_reduce(brow[:, 0], behind, AX_X, ALU.add))
            for k in range(2):
                link(dve.tensor_tensor(behind[:, k], behind[:, k],
                                       blocks[0:1, k].unsqueeze(1).to_broadcast([1, NBLK, E]), ALU.mult))
            link(dve.tensor_reduce(brow[:, 1], behind, AX_X, ALU.add))
            flat_row = [brow[:, i].rearrange("o k b -> o (k b)") for i in range(2)]
            link(dve.tensor_scalar(blk_exp_w, flat_row[0], float(E - 1), None, ALU.min))
            link(dve.tensor_copy(blk_row_w, flat_row[0]))
            link(dve.tensor_scalar(blk_row_w, blk_row_w, 1, None, ALU.bitwise_and))
            link(dve.tensor_tensor(brow[:, 1], bi, brow[:, 1], ALU.subtract))
            odd = behind.rearrange("o k b e -> o (k b e)")[:, 0:2 * NBLK]
            turn = behind.rearrange("o k b e -> o (k b e)")[:, 2 * NBLK:4 * NBLK]
            link(dve.tensor_copy(odd, blk_row_w))
            link(dve.tensor_scalar(turn, odd, float(-2 * BLK), float(BLK), ALU.mult, ALU.add))
            link(dve.tensor_tensor(turn, turn, flat_row[1], ALU.mult))
            link(dve.scalar_tensor_tensor(out=turn, in0=odd, scalar=float(PAIR - BLK - PAIR // 2), in1=turn,
                                          op0=ALU.mult, op1=ALU.add))
            link(dve.scalar_tensor_tensor(out=blk_row_w, in0=flat_row[0], scalar=float(PAIR // 2), in1=turn,
                                          op0=ALU.mult, op1=ALU.add))
            dve.tensor_copy(pad_row[:, :], start[0:1, :, :].rearrange("p k e -> p (k e)")).then_inc(table_ready, 1)
            dve.wait_ge(w_loaded[2], 16 * 6)

            for k in range(2):
                def moe_tick(u):
                    lo, hi = k * NBLK, (k + 1) * NBLK
                    b = u.back(1)
                    if b.active(hi, lo):
                        dve.wait_ge(mt_hi, b.n(1))
                        dve.tensor_tensor(tS[b.par()][:, 1, :, 0:BLK],
                                          D0[:, b.par() * 512:(b.par() + 1) * 512].rearrange("p (c n) -> p c n", c=KC),
                                          tS[b.par()][:, 0, :, 0:BLK], ALU.subtract).then_inc(mt_lo, 1)
                    b = u.back(2)
                    if b.active(hi, lo):
                        dve.wait_ge(mh_gelu, b.n(1))
                        dve.tensor_tensor(hS[:, b.par(), 1], hid[:, 2 * b.par():2 * b.par() + 2, 0:BLK],
                                          hS[:, b.par(), 0], ALU.subtract).then_inc(mh_lo, 1)
                    b = u.back(3)
                    if b.active(hi, lo):
                        e = dve.value_load(blk_exp[0:1, ds(b.n(), 1)], min_val=0, max_val=E - 1)
                        dve.wait_ge(m2_done, b.n(1))
                        if b.has(NY):
                            dve.wait_ge(y_scattered[b.off % NY], b.same(16 * TB, NY))
                        y = y_out[b.off % NY]
                        dve.scalar_tensor_tensor(
                            out=y, in0=D2[:, b.par() * 512:(b.par() + 1) * 512].rearrange("p (j n) -> p j n", j=TB),
                            scalar=1 / WS, in1=m_b2[:, ds(e * D, D)].unsqueeze(1).to_broadcast([P, TB, D]),
                            op0=ALU.mult, op1=ALU.add).then_inc(y_scaled, 1)
                        dve.wait_ge(y_scaled, b.n(1))
                        if k == 1:
                            loaded = b.n(NROW - b.off % NROW - NBLK, 16 // NROW)
                            dve.wait_ge(partial_loaded[b.off % NROW], loaded)
                        w = (W1C, W2C)[k]
                        for j in range(TB):
                            row = row_in[b.off % NROW][:, j]
                            last = dve.scalar_tensor_tensor(out=y[:, j], in0=y[:, j], scalar=row[:, w:w + 1],
                                                            in1=row[:, RES:ROW1], op0=ALU.mult, op1=ALU.add)
                        last.then_inc(y_ready, 1)
                    b = u
                    if b.active(hi, lo):
                        dve.wait_ge(mt_loaded[b.off % NROW], b.same_done(16, NROW))
                        dve.tensor_copy(idx[:, b.off % NROW], row_in[b.off % NROW][:, :, (NEXT, ID)[k]]).then_inc(idx_ready, 1)

                pipeline(dve, NBLK, 6, moe_tick, 8, start=k * NBLK, step=NROW)

        @block.tensor
        def _(pe):
            dve_n = [0]

            def dve_step():
                dve_n[0] += 1
                pe.wait_ge(eig_dve, dve_n[0])

            pe.wait_ge(const_ready, 1)
            pe.wait_ge(w_loaded[0], 16)
            pe.transpose(D3[:, 0:P], A[:, :], ident[:, :]).then_inc(eig_pe, 1)
            dve_step()
            pe.wait_ge(eig_act, 1)
            pe.transpose(D3[0:1, P:2 * P], tiny[:, 0:1], ident[:, :]).then_inc(eig_pe, 1)
            dve_step()
            pe.matmul(D3[:, 256:257], ones[0:1, :], tiny[0:1, 2:3], start=True, stop=True).then_inc(eig_pe, 1)
            dve_step()
            for i in range(SQUARINGS):
                s = sq[:, i % 2]
                pe.matmul(D2[:, (i % 2) * 512:(i % 2) * 512 + P], s, s, start=True, stop=True).then_inc(eig_pe, 1)
                dve_step()
                if i % NORM_EVERY == NORM_EVERY - 1:
                    pe.matmul(D3[:, 256:257], ones[:, :], tiny[:, 5:6], start=True, stop=True)\
                      .then_inc(eig_pe, 1)
                    dve_step()
            dve_step()
            pe.matmul(D3[:, 256:258], ones[:, :], tiny[:, 8:10], start=True, stop=True).then_inc(eig_pe, 1)

            def transposed(src, bank, g=None, halves=None):
                for j in range(T):
                    if halves is not None and j % 2 == 0:
                        pe.wait_ge(halves, g.n(0, 2, j // 2 + 1))
                    for c in range(KC):
                        last = pe.transpose(bank[:, c * GT + j * P:c * GT + (j + 1) * P],
                                            src[:, j, c * P:(c + 1) * P], ident[:, :])
                return last

            def project(bank, lhs, w, chunks, tiles=range(T)):
                for j in tiles:
                    for c in range(chunks):
                        last = pe.matmul(bank[:, j * D:(j + 1) * D], lhs[:, c, j * P:(j + 1) * P], w[:, c],
                                         start=(c == 0), stop=(c == chunks - 1))
                return last

            def split_cols(bank, w, col, parts):
                for m in range(2):
                    n = 0
                    for a, b in PARTS:
                        for c in range(KC):
                            last = pe.matmul(bank[:, m * GT:(m + 1) * GT],
                                             w[:, a, c, col + m * P:col + (m + 1) * P], parts[:, b, c],
                                             start=(n == 0), stop=(n == len(PARTS) * KC - 1))
                            n += 1
                return last

            def split_rows(bank, w, parts):
                for j in range(T):
                    n = 0
                    for a, b in PARTS:
                        for c in range(KC):
                            last = pe.matmul(bank[:, j * D:(j + 1) * D], parts[:, b, c, j * P:(j + 1) * P],
                                             w[:, a, c], start=(n == 0), stop=(n == len(PARTS) * KC - 1))
                            n += 1
                return last

            def scores(g, jj):
                if jj == 0:
                    if g.has(1):
                        pe.wait_ge(yb_ready, g.n(0, 2))
                    pe.wait_ge(q_ready, g.n(1))
                    pe.wait_ge(k_ready, g.n(1))
                else:
                    pe.wait_ge(sc_capped[0], g.n(1))
                q, k = qT, kT
                for j in range(2):
                    tok = slice((2 * jj + j) * P, (2 * jj + j + 1) * P)
                    for m in range(KC):
                        for r in range(2):
                            col = (r * 4 + j * 2 + m) * P
                            last = pe.matmul(D1[:, col:col + P], q[r * HD:(r + 1) * HD, m, tok],
                                             k[r * HD:(r + 1) * HD, m, tok], start=True, stop=True)
                last.then_inc(sc_done[jj], 1)

            def turn_probs(g, jj):
                pe.wait_ge(prob_ready[jj], g.n(1))
                if jj == 0:
                    if g.has(2):
                        pe.wait_ge(count_ready, g.n(-1))
                else:
                    pe.wait_ge(oT_ready[0], g.n(1))
                for i in range(8):
                    last = pe.transpose(D2[:, i * P:(i + 1) * P], prob[:, jj, i], ident[:, :])
                    if i % 4 == 3:
                        last.then_inc(pT_done[jj], 1)

            def mix_values(g, jj):
                pe.wait_ge(v_ready, g.n(1))
                for r in range(2):
                    pe.wait_ge(pT_ready[jj], g.n(0, 2, r + 1))
                    for j in range(2):
                        for m in range(H // 2):
                            h, col = 2 * m + r, m * 256 + j * P
                            last = pe.matmul(D2[r * HD:(r + 1) * HD, col:col + P],
                                             v[:, g.par(), 2 * jj + j, h * HD:(h + 1) * HD],
                                             pT[:, r * 4 + j * 2 + m], start=True, stop=True)
                last.then_inc(pv_done[jj], 1)

            def tick(u):
                m0, m1, m2, m3, m4 = (u.back(k) for k in range(5))
                if m2.active(NG):
                    scores(m2, 0)
                if m3.active(NG):
                    if m3.has(1):
                        pe.wait_ge(zb_ready, m3.n(0, 2))
                    transposed(x2[:, m3.par()], D3, m3, x2_ready).then_inc(x2T_done, 1)
                if m4.active(NG):
                    pe.wait_ge(t_ready, m4.n(1))
                    pe.wait_ge(oT_ready[1], m4.n(2) if m4.reg is not None else min(m4.off + 2, NG))
                    transposed(row_out[:, m4.par()], D2).then_inc(tT_done, 1)
                if m1.active(NG):
                    pe.wait_ge(x0_ready, m1.n(1))
                    if m1.has(1):
                        pe.wait_ge(v_ready, m1.n())
                    for c in range(KC):
                        for j in range(T):
                            last = pe.matmul(D0[:, c * GT + j * P:c * GT + (j + 1) * P],
                                             x0[:, m1.par(), j, c * P:(c + 1) * P], LT[:, :],
                                             start=True, stop=True)
                    last.then_inc(xp_done, 1)
                if m4.active(NG):
                    pe.wait_ge(tT_ready, m4.n(1))
                    for j in range(T):
                        for c in range(KC):
                            last = pe.matmul(D2[:, j * E:(j + 1) * E], tT[:, c, j * P:(j + 1) * P], w_r[:, c],
                                             start=(c == 0), stop=(c == KC - 1))
                    last.then_inc(lg_done, 1)
                if m3.active(NG):
                    pe.wait_ge(x2lo_ready, m3.n(1))
                    split_cols(D3, w_f1, 0, x2s).then_inc(f1_done[0], 1)
                if m1.active(NG):
                    pe.wait_ge(xplo_ready, m1.n(1))
                    split_rows(D0, w_c, xps).then_inc(h_done, 1)
                if m3.active(NG):
                    pe.wait_ge(hid_ready[0], m3.n(1))
                    split_cols(D3, w_f1, 2 * P, x2s).then_inc(f1_done[1], 1)
                if m4.active(NG):
                    pe.wait_ge(picked_ready, m4.n(1))
                    for j in range(T):
                        for i in range(j + 1):
                            pe.matmul(D2[:, 512 + j * 2 * E:512 + (j + 1) * 2 * E],
                                      ones_h[:, :] if i < j else before_h[:, :], picked[:, i],
                                      start=(i == 0), stop=(i == j))
                    for i in range(T):
                        last = pe.matmul(D2[:, 512 + T * 2 * E:512 + (T + 1) * 2 * E], ones_h[:, :], picked[:, i],
                                         start=(i == 0), stop=(i == T - 1))
                    last.then_inc(rank_done, 1)
                if m2.active(NG):
                    scores(m2, 1)
                    turn_probs(m2, 0)
                if m3.active(NG):
                    pe.wait_ge(hid_ready[1], m3.n(1))
                    project(D3, hid, w_f2, HC, (0, 1))
                    project(D3, hid, w_f2, HC, (2,))
                    project(D3, hid, w_f2, HC, (3,)).then_inc(f2_done, 1)
                if m2.active(NG):
                    mix_values(m2, 0)
                if m1.active(NG):
                    transposed(x1[:, m1.par()], D0, m1, x1_ready).then_inc(x1T_done, 1)
                if m2.active(NG):
                    turn_probs(m2, 1)
                    mix_values(m2, 1)
                if m1.active(NG):
                    pe.wait_ge(x1lo_ready, m1.n(1))
                    split_cols(D0, w_qkv[:, 0], 0, x1s).then_inc(q_done, 1)
                if m2.active(NG):
                    pe.wait_ge(oT_ready[1], m2.n(1))
                    pe.wait_ge(sc_capped[1], m2.n(1))
                    project(D1, oT, w_o, KC).then_inc(wo_done, 1)
                if m1.active(NG):
                    pe.wait_ge(q_ready, m1.n(1))
                    split_cols(D0, w_qkv[:, 1], 0, x1s).then_inc(k_done, 1)
                    pe.wait_ge(k_ready, m1.n(1))
                    split_rows(D0, w_qkv[:, 2], x1s).then_inc(v_done, 1)

            pe.wait_ge(lt_ready, 1)
            pe.wait_ge(w_loaded[1], 16 * 10)
            pe.wait_ge(w_loaded[2], 16 * 6)
            pe.wait_ge(stage_lo, len(JOBS))
            pipeline(pe, NG, 5, tick, 6)

            pe.wait_ge(table_ready, 1)
            ES = 2 * KC * D

            for k in range(2):
                def moe_tick(u):
                    lo, hi = k * NBLK, (k + 1) * NBLK
                    b = u.back(1)
                    if b.active(hi, lo):
                        pe.wait_ge(mt_loaded[b.off % NROW], b.same_done(16, NROW))
                        for c in range(KC):
                            for j in range(TB):
                                last = pe.transpose(D0[:, b.par() * 512 + c * BLK + j * P:
                                                       b.par() * 512 + c * BLK + (j + 1) * P],
                                                    row_in[b.off % NROW][:, j, c * P:(c + 1) * P], ident[:, :])
                        last.then_inc(mt_done, 1)
                    b = u.back(2)
                    if b.active(hi, lo):
                        e = pe.value_load(blk_exp[0:1, ds(b.n(), 1)], min_val=0, max_val=E - 1)
                        pe.wait_ge(mt_hi, b.n(1))
                        for m in range(KC):
                            n = 0
                            for a, p in PARTS:
                                if m == 0 and p == 1:
                                    pe.wait_ge(mt_lo, b.n(1))
                                for c in range(KC):
                                    last = pe.matmul(D1[:, b.par() * 512 + m * BLK:b.par() * 512 + (m + 1) * BLK],
                                                     m_w1[:, ds(e * ES + (a * KC + c) * D + m * P, P)],
                                                     tS[b.par()][:, p, c, 0:BLK],
                                                     start=(n == 0), stop=(n == len(PARTS) * KC - 1))
                                    n += 1
                        last.then_inc(m1_done, 1)
                    b = u.back(3)
                    if b.active(hi, lo):
                        e = pe.value_load(blk_exp[0:1, ds(b.n(), 1)], min_val=0, max_val=E - 1)
                        pe.wait_ge(mh_hi, b.n(1))
                        if b.has(2):
                            pe.wait_ge(y_ready, b.n(-1))
                        for j in range(TB):
                            n = 0
                            for a, p in PARTS:
                                if j == 0 and p == 1:
                                    pe.wait_ge(mh_lo, b.n(1))
                                for c in range(KC):
                                    last = pe.matmul(D2[:, b.par() * 512 + j * D:b.par() * 512 + (j + 1) * D],
                                                     hS[:, b.par(), p, c, j * P:(j + 1) * P],
                                                     m_w2[:, ds(e * ES + (a * KC + c) * D, D)],
                                                     start=(n == 0), stop=(n == len(PARTS) * KC - 1))
                                    n += 1
                        last.then_inc(m2_done, 1)

                pipeline(pe, NBLK, 6, moe_tick, 8, start=k * NBLK, step=NROW)


_INS = ['x', 'adj', 'L0_gnn_Wc', 'L0_gnn_bc', 'L0_gnn_g1', 'L0_gnn_be1', 'L0_gnn_Wq', 'L0_gnn_Wk', 'L0_gnn_Wv',
        'L0_gnn_Wo', 'L0_gnn_bo', 'L0_gnn_g2', 'L0_gnn_be2', 'L0_gnn_W1', 'L0_gnn_b1', 'L0_gnn_W2', 'L0_gnn_b2',
        'L0_gnn_g3', 'L0_gnn_be3', 'L0_ffn_router_w', 'L0_ffn_w1', 'L0_ffn_b1', 'L0_ffn_w2', 'L0_ffn_b2']


def kernel(**inputs):
    import numpy as _np
    import concourse.bacc as _bacc
    from concourse import mybir as _mybir
    from concourse.bass_utils import run_bass_kernel_spmd as _run

    nc = _bacc.Bacc("TRN2", target_bir_lowering=False, num_devices=1)
    arrays, args = {}, []
    for name in _INS:
        a = _np.ascontiguousarray(inputs[name])
        arrays[f"in_{name}_dram"] = a
        args.append(nc.dram_tensor(f"in_{name}_dram", a.shape, _mybir.dt.from_np(a.dtype), kind="ExternalInput").ap())
    shape = inputs['x'].shape
    args.append(nc.dram_tensor("out_0_dram", shape, _mybir.dt.float32, kind="ExternalOutput").ap())
    build_program(nc, *args)
    r = _run(nc, [arrays], core_ids=[0])
    return r.results[0]["out_0_dram"]
```
